# Optimizing a Trainium2 kernel written in Bass

```python
import numpy as np
import jax
import jax.numpy as jnp

def _softmax(x, axis=-1):
    return jax.nn.softmax(x, axis=axis)

def _gelu(x):
    return jax.nn.gelu(x, approximate=True)

def _silu(x):
    return jax.nn.silu(x)

def _sigmoid(x):
    return jax.nn.sigmoid(x)

def _layernorm(x, axis=-1, eps=1e-05):
    m = jnp.mean(x, axis=axis, keepdims=True)
    v = jnp.var(x, axis=axis, keepdims=True)
    return (x - m) / jnp.sqrt(v + eps)

def _scatter_add(tgt, idx, src, axis=0):
    return tgt.at[idx].add(src)

def _segment_sum(src, seg, n):
    return jax.ops.segment_sum(src, seg, n)
kernel_name = 'mk_decoder_preln_d1_seqx_r4_79855b'

def setup_inputs(seed: int=0):
    np.random.seed(seed)
    _w = jnp.asarray

    def _rec_inputs():
        import jax
        import jax.numpy as jnp
        _rk = jax.random.key(seed)
        x = -0.0003929 + 0.9999 * jax.random.normal(jax.random.fold_in(_rk, 1), (16, 128, 256), jnp.float32)
        _lenS = 128 - jax.random.randint(jax.random.fold_in(_rk, 7), (16,), 0, max(1, 128 // 4) + 1, jnp.int32)
        _lenS2 = 128 - jax.random.randint(jax.random.fold_in(_rk, 8), (16,), 0, max(1, 128 // 4) + 1, jnp.int32)
        _ctx_1024P = jax.random.normal(jax.random.fold_in(_rk, 11), (16, 16, 256), jnp.float32)
        _ctx_1024c = jax.random.dirichlet(jax.random.fold_in(_rk, 511), 0.3 * jnp.ones((16,), jnp.float32), (16, 128))
        _ctx_1024t = jnp.einsum('bsk,bkd->bsd', _ctx_1024c, _ctx_1024P)
        _ctx_1024t = _ctx_1024t * jax.lax.rsqrt(jnp.mean(jnp.square(_ctx_1024t)) + 1e-12) * 0.953939
        ctx_1024 = 2.81802e-05 + 1.00001 * (_ctx_1024t + 0.3 * jax.random.normal(jax.random.fold_in(_rk, 611), (16, 128, 256), jnp.float32))
        return (x, ctx_1024)
    x, ctx_1024 = _rec_inputs()

    def _L0_attn_setup():
        import jax, jax.numpy as jnp
        import numpy as np
        B, T, D = (4, 512, 256)
        H, DK, DV = (8, 128, 128)

        def _l2norm(u, eps=1e-12):
            n = jnp.sqrt(jnp.sum(u * u, axis=-1, keepdims=True))
            return u / jnp.maximum(n, eps)
        key = jax.random.key(seed)
        ks = jax.random.split(key, 6)
        s = 0.02
        x = jax.random.normal(ks[0], (B, T, D), dtype=jnp.float32)
        Wq = jax.random.normal(ks[1], (D, H * DK), dtype=jnp.float32) * s
        Wk = jax.random.normal(ks[2], (D, H * DK), dtype=jnp.float32) * s
        Wv = jax.random.normal(ks[3], (D, H * DV), dtype=jnp.float32) * s
        Wg = jax.random.normal(ks[4], (D, H * DK), dtype=jnp.float32) * s
        Wo = jax.random.normal(ks[5], (H * DV, D), dtype=jnp.float32) * s
        return {'x': x, 'Wq': Wq, 'Wk': Wk, 'Wv': Wv, 'Wg': Wg, 'Wo': Wo}
    _L0_attn_all = _L0_attn_setup()
    _L0_attn_in = {k: v for k, v in _L0_attn_all.items() if k in ('Wq', 'Wk', 'Wv', 'Wg', 'Wo')}
    del _L0_attn_all

    def _L0_xattn_setup():
        import jax, jax.numpy as jnp
        import numpy as np
        B, S, T = (8, 512, 512)
        D_SRC, D_TGT = (256, 256)
        key = jax.random.key(seed)
        k1, k2, k3 = jax.random.split(key, 3)
        X_src = jax.random.normal(k1, (B, S, D_SRC), dtype=jnp.float32)
        X_tgt = jax.random.normal(k2, (B, T, D_TGT), dtype=jnp.float32)
        W = jax.random.normal(k3, (D_SRC, D_TGT), dtype=jnp.float32) * (1.0 / np.sqrt(D_TGT))
        return {'X_src': X_src, 'X_tgt': X_tgt, 'W': W}
    _L0_xattn_all = _L0_xattn_setup()
    _L0_xattn_in = {k: v for k, v in _L0_xattn_all.items() if k in ('W',)}
    del _L0_xattn_all

    def _L0_ffn_setup():
        import jax, jax.numpy as jnp
        import numpy as np
        TOP_K = 2
        key = jax.random.key(seed)
        ks = jax.random.split(key, 6)
        B, S, D, BN, E = (32, 512, 256, 64, 8)
        return {'x': jax.random.normal(ks[0], (B, S, D), dtype=jnp.float32), 'gate_w': jax.random.normal(ks[1], (E, D), dtype=jnp.float32) * 0.02, 'down_w': jax.random.normal(ks[2], (E, BN, D), dtype=jnp.float32) * 0.02, 'down_b': jax.random.normal(ks[3], (E, BN), dtype=jnp.float32) * 0.02, 'up_w': jax.random.normal(ks[4], (E, D, BN), dtype=jnp.float32) * 0.02, 'up_b': jax.random.normal(ks[5], (E, D), dtype=jnp.float32) * 0.02}
    _L0_ffn_all = _L0_ffn_setup()
    _L0_ffn_in = {k: v for k, v in _L0_ffn_all.items() if k in ('gate_w', 'down_w', 'down_b', 'up_w', 'up_b')}
    del _L0_ffn_all
    return {'x': x, 'ctx_1024': ctx_1024, 'L0_attn_Wq': _L0_attn_in['Wq'], 'L0_attn_Wk': _L0_attn_in['Wk'], 'L0_attn_Wv': _L0_attn_in['Wv'], 'L0_attn_Wg': _L0_attn_in['Wg'], 'L0_attn_Wo': _L0_attn_in['Wo'], 'L0_xattn_W': _L0_xattn_in['W'], 'L0_ffn_gate_w': _L0_ffn_in['gate_w'], 'L0_ffn_down_w': _L0_ffn_in['down_w'], 'L0_ffn_down_b': _L0_ffn_in['down_b'], 'L0_ffn_up_w': _L0_ffn_in['up_w'], 'L0_ffn_up_b': _L0_ffn_in['up_b']}

def reference(x, ctx_1024, L0_attn_Wq, L0_attn_Wk, L0_attn_Wv, L0_attn_Wg, L0_attn_Wo, L0_xattn_W, L0_ffn_gate_w, L0_ffn_down_w, L0_ffn_down_b, L0_ffn_up_w, L0_ffn_up_b):
    import jax
    import jax.numpy as jnp

    def _L0_attn_ref(x, Wq, Wk, Wv, Wg, Wo):
        import jax, jax.numpy as jnp
        import numpy as np
        B, T, D = (4, 512, 256)
        H, DK, DV = (8, 128, 128)

        def _l2norm(u, eps=1e-12):
            n = jnp.sqrt(jnp.sum(u * u, axis=-1, keepdims=True))
            return u / jnp.maximum(n, eps)
        Bb, Tt, _ = x.shape
        q = _l2norm((x @ Wq).reshape(Bb, Tt, H, DK))
        k = _l2norm((x @ Wk).reshape(Bb, Tt, H, DK))
        v = (x @ Wv).reshape(Bb, Tt, H, DV)
        alpha = jax.nn.sigmoid(x @ Wg).reshape(Bb, Tt, H, DK)

        def step(S, qkva):
            q_t, k_t, v_t, a_t = qkva
            S = a_t[..., None] * S + k_t[..., None] * v_t[:, :, None, :]
            o_t = jnp.einsum('bhkv,bhk->bhv', S, q_t)
            return (S, o_t)
        S0 = jnp.zeros((Bb, H, DK, DV), dtype=x.dtype)
        xs = (q.swapaxes(0, 1), k.swapaxes(0, 1), v.swapaxes(0, 1), alpha.swapaxes(0, 1))
        _, o = jax.lax.scan(step, S0, xs)
        o = o.swapaxes(0, 1).reshape(Bb, Tt, H * DV)
        return o @ Wo

    def _L0_xattn_ref(X_src, X_tgt, W):
        import jax, jax.numpy as jnp
        import numpy as np
        B, S, T = (8, 512, 512)
        D_SRC, D_TGT = (256, 256)
        X_tgt_proj = jnp.einsum('btd,sd->bts', X_tgt, W)
        scores = jnp.einsum('bsd,btd->bst', X_src, X_tgt_proj)
        alpha = jax.nn.softmax(scores, axis=-1)
        return jnp.einsum('bst,btd->bsd', alpha, X_tgt)

    def _L0_ffn_ref(x, gate_w, down_w, down_b, up_w, up_b):
        import jax, jax.numpy as jnp
        import numpy as np
        TOP_K = 2
        pooled = x.mean(axis=1)
        gate = jax.nn.softmax(pooled @ gate_w.T, axis=-1)
        top_w, top_i = jax.lax.top_k(gate, TOP_K)
        top_w = top_w / (top_w.sum(axis=-1, keepdims=True) + 1e-08)
        Wd = down_w[top_i]
        bd = down_b[top_i]
        Wu = up_w[top_i]
        bu = up_b[top_i]
        h = jax.nn.gelu(jnp.einsum('bsd,bkcd->bksc', x, Wd) + bd[:, :, None, :], approximate=False)
        h = h * top_w[:, :, None, None]
        out = jnp.einsum('bksc,bkdc->bsd', h, Wu)
        out = out + (top_w[:, :, None] * bu).sum(axis=1)[:, None, :]
        return out
    x = x + _L0_attn_ref(_layernorm(x, axis=-1), L0_attn_Wq, L0_attn_Wk, L0_attn_Wv, L0_attn_Wg, L0_attn_Wo)
    x = x + _L0_xattn_ref(_layernorm(x, axis=-1), ctx_1024, L0_xattn_W)
    x = x + _L0_ffn_ref(_layernorm(x, axis=-1), L0_ffn_gate_w, L0_ffn_down_w, L0_ffn_down_b, L0_ffn_up_w, L0_ffn_up_b)
    return x

_drawn_inputs = setup_inputs


def setup_inputs(seed=0):
    import zlib

    import numpy as np

    out = dict(_drawn_inputs(seed))
    spreads = {}
    factors = {'L0_attn_Wg': 22.992,
     'L0_ffn_gate_w': 4.259,
     'L0_ffn_down_w': 4.481,
     'L0_ffn_down_b': 8.0,
     'L0_ffn_up_w': 4.363,
     'L0_ffn_up_b': 5.885}
    for name, (base, spread) in spreads.items():
        noise = np.random.default_rng([zlib.crc32(name.encode()), seed]).standard_normal(out[name].shape)
        drawn = base * np.exp(spread * noise) if base else spread * noise
        out[name] = jnp.asarray(drawn.astype(out[name].dtype))
    for name, factor in factors.items():
        out[name] = (out[name] * factor).astype(out[name].dtype)
    return out
```

```python
from contextlib import ExitStack

import numpy as np

import concourse.bass as bass
from concourse import mybir

P = 128
F32 = mybir.dt.float32
I32 = mybir.dt.int32
U32 = mybir.dt.uint32
ALU = mybir.AluOpType
ACT = mybir.ActivationFunctionType
AX = mybir.AxisListType.X

LN_EPS = 1e-5
NORM_EPS = 1e-12
TOPW_EPS = 1e-8
LEVELS = 7
BLOCK = 32
OUTER = LEVELS - 1
INNER = 5


def shape_constants(sequences):
    ident = np.eye(P, dtype=np.float32)
    s = np.arange(P)[:, None] % BLOCK
    t = np.arange(BLOCK)[None, :]
    owned = [s == t] + [((s >> (l + 1)) == (t >> (l + 1))) & ((s >> l) % 2 == 0) & ((t >> l) % 2 == 1)
                        for l in range(INNER)]
    owned = np.stack([np.tile(m, (1, sequences)) for m in owned], axis=1).astype(np.float32)
    experts = np.broadcast_to(np.arange(8, dtype=np.float32), (P, 8)).copy()
    return ident, owned, experts


def decoder_kernel(nc, x, ctx, ctxT, wq, wk, wv, wg, wo, xwT, gateT, downT, down_b, up, up_b,
                   ident_c, owned_c, experts_c, out):
    B, T, D = x.shape
    H = wq.shape[1] // P
    KC = D // P
    GB = 4
    NG = B // GB
    N = GB * T
    E = gateT.shape[1]
    EJ = downT.shape[1] // P
    assert T == P and D == 256 and N == 512 and E == 8

    with ExitStack() as stack:
        def sb(name, shape, dt=F32):
            return stack.enter_context(nc.sbuf_tensor(name, shape, dt))

        def bank(name):
            return stack.enter_context(nc.psum_tensor(name, [P, 512], F32))

        def sem(name):
            return stack.enter_context(nc.semaphore(name))

        wq_sb, wk_sb, wv_sb, wg_sb = (sb(n, [P, KC, H * P]) for n in ("wq_sb", "wk_sb", "wv_sb", "wg_sb"))
        wo_sb = sb("wo_sb", [P, H, D])
        xw_sb = sb("xw_sb", [P, KC, D])
        gate_sb = sb("gate_sb", [P, KC, E])
        down_sb = sb("down_sb", [P, KC, EJ * P])
        downb_sb = sb("downb_sb", [P, EJ])
        up_sb = sb("up_sb", [P, EJ, D])
        upb_sb = sb("upb_sb", [E, D])
        ident = sb("ident", [P, P])
        N_IN = GB * BLOCK
        owned = sb("owned", [P, 1 + INNER, N_IN])
        experts = sb("experts", [P, E])
        ones = sb("ones", [P, 2])
        scratch = sb("scratch", [P, 1])
        pool_scratch = sb("pool_scratch", [P, 1])
        neg_half = sb("neg_half", [P, 8])
        x_next = sb("x_next", [P, GB, D])
        x_res = sb("x_res", [P, GB, D])
        ctx_sb = sb("ctx_sb", [P, GB, D])
        ctxT_sb = sb("ctxT_sb", [P, KC, GB, T])
        stats = sb("stats", [P, GB, 6])
        mean_var = sb("mean_var", [P, GB, 2])
        var_eps = sb("var_eps", [P, GB])
        rstd = sb("rstd", [P, GB])
        xn = sb("xn", [P, GB, D])
        xnT = sb("xnT", [P, KC, N])
        alpha = sb("alpha", [P, 2, N])
        q_raw = sb("q_raw", [P, 2, N])
        qk_dec = sb("qk_dec", [P, 2, 2, N])
        squares = sb("squares", [P, 2, N])
        spans = sb("spans", [P, N])
        norm_sq = sb("norm_sq", [P, 2, GB])
        rnorm = sb("rnorm", [P, 2, 2, GB])
        v_sb = sb("v_sb", [P, 2, GB, P])
        by_level = sb("by_level", [P, 1 + INNER, GB, BLOCK])
        blocks = sb("blocks", [P, GB, BLOCK])
        attnT = sb("attnT", [P, GB, T])
        o_sb = sb("o_sb", [P, GB, P])
        oT_sb = sb("oT_sb", [P, H, N])
        x_mid = sb("x_mid", [P, GB, D])
        xnT2 = sb("xnT2", [P, KC, N])
        projT = sb("projT", [P, KC, GB, T])
        neg_max = sb("neg_max", [P, GB])
        probs = sb("probs", [P, GB, T])
        prob_sum = sb("prob_sum", [P, GB])
        prob_rsum = sb("prob_rsum", [P, GB])
        probsT = sb("probsT", [P, GB, T])
        pooled = sb("pooled", [P, KC * GB])
        logits = sb("logits", [P, GB, E])
        gate_max = sb("gate_max", [P, GB])
        gate_exp = sb("gate_exp", [P, GB, E])
        gate_sum = sb("gate_sum", [P, GB])
        top_val = sb("top_val", [P, GB, 8])
        top_idx = sb("top_idx", [P, GB, 8], U32)
        top_num = sb("top_num", [P, GB, 8])
        is_first = sb("is_first", [P, GB, E])
        is_second = sb("is_second", [P, GB, E])
        top_sum = sb("top_sum", [P, GB])
        weight = sb("weight", [P, GB, E])
        weight_col = sb("weight_col", [P, EJ, GB])
        weightT = sb("weightT", [E, GB, T])
        hidden = sb("hidden", [P, EJ, N])
        out_sb = sb("out_sb", [P, GB, D])

        bank_q, bank_k, bank_gv, bank_lo, bank_hi, bank_o, tail0, tail1 = (
            bank(n) for n in ("bank_q", "bank_k", "bank_gv", "bank_lo", "bank_hi", "bank_o", "tail0", "tail1"))
        tails = (tail0, tail1)

        w_in, c_in, x_in, ctx_in, out_free = (sem(n) for n in ("w_in", "c_in", "x_in", "ctx_in", "out_free"))
        consts_set = sem("consts_set")
        g_mm, q_mm, k_mm, v_mm, norm_mm, level_mm, o_mm, oT_mm = (
            sem(n) for n in ("g_mm", "q_mm", "k_mm", "v_mm", "norm_mm", "level_mm", "o_mm", "oT_mm"))
        tail_mm = (sem("tail_mm0"), sem("tail_mm1"))
        tail_free = (sem("tail_free0"), sem("tail_free1"))
        alpha_set, q_set, k_set, oT_set, attnT_set = (
            sem(n) for n in ("alpha_set", "q_set", "k_set", "oT_set", "attnT_set"))
        gate_exp_set = sem("gate_exp_set")
        level0_set, decayed, span_set, masked, blocks_set, norm_sq_set, v_set, o_set = (
            sem(n) for n in ("level0_set", "decayed", "span_set", "masked", "blocks_set", "norm_sq_set", "v_set", "o_set"))
        ln_stat, ln_var, ln_out = sem("ln_stat"), sem("ln_var"), sem("ln_out")
        ln_rstd, rnorm_set, x_res_set = sem("ln_rstd"), sem("rnorm_set"), sem("x_res_set")
        row_stat, max_set, pooled_set, gate_max_set, logits_set, small, weighted = (
            sem(n) for n in ("row_stat", "max_set", "pooled_set", "gate_max_set", "logits_set", "small", "weighted"))

        (WO0, WO1, PROJ0, PROJ1, XT0, XT1, X2T0, X2T1, SCORES, PT, AV0, AV1, X3T0, X3T1,
         GATE, H0, H1, H2, H3, WT, UP0, UP1) = range(22)

        def fills(i, f):
            if isinstance(i, int) and i == 0:
                return 0
            return 11 * i - 10 + f // 2 - (1 if isinstance(i, int) and i == NG and f > XT1 else 0)

        def norms_done(i, k):
            if isinstance(i, int) and i == 0:
                return 0
            return 3 * i - 2 + k - (1 if isinstance(i, int) and i == NG else 0)

        def positive(engine, s, value):
            if not isinstance(value, int) or value > 0:
                engine.wait_ge(s, value)

        def view(tensor, start, dims):
            whole = tensor[:]
            return bass.AP(whole.tensor, whole.offset + start, [list(whole.ap[0])] + dims)

        N_W, N_C = 16 * 11, 16 * 3

        block = stack.enter_context(nc.Block())

        @block.sync
        def _(sp):
            def load_x(i):
                sp.dma_start(x_next[:], x[bass.ts(i, GB)].rearrange("b t d -> t b d")).then_inc(x_in, 16)

            def load_ctx(i):
                for c in range(KC):
                    sp.dma_start(ctxT_sb[:, c], ctxT[bass.ts(i, GB), P * c:P * c + P].rearrange("b p t -> p b t")
                                 ).then_inc(ctx_in, 16)

            def load_ctx2(i):
                sp.dma_start(ctx_sb[:], ctx[bass.ts(i, GB)].rearrange("b t d -> t b d")).then_inc(ctx_in, 16)

            load_x(0)
            for dst, src in ((ident, ident_c), (owned, owned_c), (experts, experts_c)):
                sp.dma_start(dst[:], src).then_inc(c_in, 16)
            for dst, src in ((wg_sb, wg), (wq_sb, wq), (wk_sb, wk), (wv_sb, wv)):
                sp.dma_start(dst[:], src.rearrange("(c p) n -> p c n", p=P)).then_inc(w_in, 16)
            load_ctx(0)
            load_ctx2(0)
            sp.dma_start(wo_sb[:], wo.rearrange("(h p) n -> p h n", p=P)).then_inc(w_in, 16)
            for dst, src in ((xw_sb, xwT), (gate_sb, gateT), (down_sb, downT)):
                sp.dma_start(dst[:], src.rearrange("(c p) n -> p c n", p=P)).then_inc(w_in, 16)
            sp.dma_start(downb_sb[:], down_b).then_inc(w_in, 16)
            sp.dma_start(up_sb[:], up.rearrange("(j p) n -> p j n", p=P)).then_inc(w_in, 16)
            sp.dma_start(upb_sb[:], up_b).then_inc(w_in, 16)
            sp.wait_ge(ln_out, 1)
            sp.wait_ge(x_res_set, 1)
            load_x(1)

            def store(i):
                for f in (UP0, UP1):
                    sp.wait_ge(tail_free[f % 2], fills(i, f) + 1)
                sp.dma_start(out[bass.ts(i - 1, GB)].rearrange("b t d -> t b d"), out_sb[:]).then_inc(out_free, 16)

            def body(i, last):
                sp.wait_ge(tail_mm[1], fills(i, PROJ1) + 1)
                load_ctx(i)
                if not last:
                    sp.wait_ge(x_res_set, i + 1)
                    sp.wait_ge(ln_out, norms_done(i, 0) + 1)
                    load_x(i + 1)
                sp.wait_ge(tail_mm[1], fills(i, AV1) + 1)
                load_ctx2(i)
                store(i)

            with sp.Fori(1, NG - 1) as i:
                body(i, False)
            body(NG - 1, True)
            store(NG)
            sp.wait_ge(out_free, 16 * (NG + 1))

        @block.gpsimd
        def _(pool):
            nc.gpsimd.memset(neg_half[:], -0.5)
            nc.gpsimd.memset(ones[:], 1.0)
            nc.gpsimd.memset(out_sb[:], 0.0).then_inc(out_free, 16)
            nc.gpsimd.memset(attnT[:], 0.0).then_inc(consts_set, 1)
            pool.wait_ge(consts_set, 1)

            def ln_power(i, k):
                pool.wait_ge(ln_var, norms_done(i, k) + 1)
                positive(pool, ln_out, norms_done(i, k))
                nc.gpsimd.tensor_tensor(rstd[:], var_eps[:], neg_half[:, 0:GB], ALU.pow).then_inc(ln_rstd, 1)

            def keep_x(i):
                pool.wait_ge(x_in, 16 * (i + 1))
                if not (isinstance(i, int) and i == 0):
                    for f in (WO0, WO1):
                        pool.wait_ge(tail_free[f], fills(i, f) + 1)
                nc.gpsimd.tensor_tensor(pool_scratch[:], neg_half[:, 0:1], neg_half[:, 0:1], ALU.mult)
                nc.gpsimd.tensor_copy(x_res[:], x_next[:]).then_inc(x_res_set, 1)

            def reciprocal_norms(n, par):
                pool.wait_ge(norm_sq_set, n + 1)
                if not (isinstance(n, int) and n < 2):
                    pool.wait_ge(v_set, n - 1)
                    pool.wait_ge(o_set, n - 1)
                nc.gpsimd.tensor_tensor(rnorm[:, par].rearrange("p a b -> p (a b)"),
                                        norm_sq[:].rearrange("p a b -> p (a b)"), neg_half[:],
                                        ALU.pow).then_inc(rnorm_set, 1)

            def body(i, tail):
                ln_power(i, 0)
                keep_x(i)
                if tail:
                    ln_power(i, 1)
                reciprocal_norms(i * H, 0)
                for h in range(H):
                    if tail and h == 4:
                        ln_power(i, 2)
                    if h < H - 1:
                        reciprocal_norms(i * H + h + 1, (h + 1) % 2)

            body(0, False)
            with pool.Fori(1, NG) as i:
                body(i, True)
            ln_power(NG, 1)
            ln_power(NG, 2)

        @block.scalar
        def _(act):
            def head_in(n, par):
                act.wait_ge(g_mm, n + 1)
                if not (isinstance(n, int) and n < 2):
                    act.wait_ge(level_mm, LEVELS * (n - 1))
                nc.scalar.activation(alpha[:, par], bank_gv[:], ACT.Sigmoid).then_inc(alpha_set, 1)
                act.wait_ge(q_mm, n + 1)
                positive(act, norm_mm, n)
                nc.scalar.copy(q_raw[:, par], bank_q[:])
                nc.scalar.activation(squares[:, 0], bank_q[:], ACT.Square).then_inc(q_set, 1)
                act.wait_ge(k_mm, n + 1)
                nc.scalar.copy(qk_dec[:, par, 1], bank_k[:])
                nc.scalar.activation(squares[:, 1], bank_k[:], ACT.Square).then_inc(k_set, 1)

            def oT_out(n, h):
                act.wait_ge(oT_mm, n + 1)
                nc.scalar.copy(oT_sb[:, h], bank_o[:]).then_inc(oT_set, 1)

            def expand(n):
                positive(act, o_mm, n)
                act.wait_ge(level_mm, LEVELS * (n + 1))
                outer = bank_o[:].rearrange("p (b t) -> p b t", b=GB)
                for r in range(3):
                    lo, t0 = BLOCK * r, BLOCK * (r + 1) if r != 1 else 2 * BLOCK
                    nc.scalar.copy(attnT[lo:lo + BLOCK, :, t0:T], outer[lo:lo + BLOCK, :, t0:T])
                act.wait_ge(blocks_set, n + 1)
                for r in range(T // BLOCK):
                    lo = BLOCK * r
                    last = nc.scalar.copy(attnT[lo:lo + BLOCK, :, lo:lo + BLOCK], blocks[lo:lo + BLOCK])
                last.then_inc(attnT_set, 1)

            def pre(i, heads, tail):
                if tail:
                    for f in (PROJ0, PROJ1):
                        act.wait_ge(tail_mm[f % 2], fills(i, f) + 1)
                        nc.scalar.copy(projT[:, f % 2].rearrange("p b t -> p (b t)"),
                                       tails[f % 2][:]).then_inc(tail_free[f % 2], 1)
                if heads:
                    for f in (XT0, XT1):
                        act.wait_ge(tail_mm[f % 2], fills(i, f) + 1)
                        nc.scalar.copy(xnT[:, f % 2], tails[f % 2][:]).then_inc(tail_free[f % 2], 1)

            def gelu(i, f):
                j = f - H0
                act.wait_ge(tail_mm[f % 2], fills(i, f) + 1)
                nc.scalar.activation(hidden[:, j], tails[f % 2][:], ACT.Gelu,
                                     bias=downb_sb[:, j:j + 1]).then_inc(tail_free[f % 2], 1)

            def tail_piece(i, s):
                if s == 1 or s == 5:
                    for f in (X2T0, X2T1) if s == 1 else (X3T0, X3T1):
                        act.wait_ge(tail_mm[f % 2], fills(i, f) + 1)
                        nc.scalar.copy(xnT2[:, f % 2], tails[f % 2][:]).then_inc(tail_free[f % 2], 1)
                if s == 2:
                    act.wait_ge(max_set, i)
                    for b in range(GB):
                        last = nc.scalar.activation(probs[:, b], tail0[:, T * b:T * b + T], ACT.Exp,
                                                    bias=neg_max[:, b:b + 1], accum_out=prob_sum[:, b:b + 1])
                    last.then_inc(tail_free[0], 1)
                if s == 3:
                    act.wait_ge(tail_mm[1], fills(i, PT) + 1)
                    nc.scalar.copy(probsT[:].rearrange("p b t -> p (b t)"), tail1[:]).then_inc(tail_free[1], 1)
                if s == 6:
                    act.wait_ge(logits_set, i)
                    nc.scalar.activation(gate_exp[:], logits[:], ACT.Exp).then_inc(gate_exp_set, 1)
                    gelu(i, H0)
                if s == 7:
                    gelu(i, H3)

            def late_piece(i, s):
                if s == 6:
                    gelu(i, H1)
                    gelu(i, H2)

            def body(i, tail):
                pre(i, True, tail)
                head_in(i * H, 0)
                for h in range(H):
                    n = i * H + h
                    if h < H - 1:
                        head_in(n + 1, (h + 1) % 2)
                    if h > 0:
                        oT_out(n - 1, h - 1)
                    if tail:
                        tail_piece(i, h)
                    expand(n)
                    if tail:
                        late_piece(i, h)
                oT_out(i * H + H - 1, H - 1)

            act.wait_ge(consts_set, 1)
            body(0, False)
            act.wait_ge(w_in, N_W)
            with act.Fori(1, NG) as i:
                body(i, True)
            pre(NG, False, True)
            for s in range(H):
                tail_piece(NG, s)
                late_piece(NG, s)

        @block.vector
        def _(dve):
            def wait_first(s, value):
                dve.wait_ge(s, value)
                nc.vector.memset(scratch[:], 0.0)

            def layernorm(i, k, src):
                base = norms_done(i, k)
                for b in range(GB):
                    last = nc.vector.bn_stats(stats[:, b], src[:, b])
                last.then_inc(ln_stat, 1)
                wait_first(ln_stat, 2 * base + 1)
                for b in range(GB):
                    last = nc.vector.bn_aggr(mean_var[:, b], stats[:, b])
                last.then_inc(ln_stat, 1)
                dve.wait_ge(ln_stat, 2 * base + 2)
                nc.vector.tensor_scalar(var_eps[:], mean_var[:, :, 1], LN_EPS, None, ALU.add).then_inc(ln_var, 1)
                dve.wait_ge(ln_rstd, base + 1)
                if k == 1 and not (isinstance(i, int) and i == NG):
                    dve.wait_ge(tail_mm[1], fills(i, XT1) + 1)
                elif k == 2:
                    dve.wait_ge(tail_mm[1], fills(i, X2T1) + 1)
                for b in range(GB):
                    last = nc.vector.tensor_scalar(xn[:, b], src[:, b], mean_var[:, b, 0:1], rstd[:, b:b + 1],
                                                   ALU.subtract, ALU.mult)
                last.then_inc(ln_out, 1)

            def q_decayed(n, par):
                dve.wait_ge(q_set, n + 1)
                dve.wait_ge(alpha_set, n + 1)
                if not (isinstance(n, int) and n < 2):
                    dve.wait_ge(level_mm, LEVELS * (n - 1))
                nc.vector.tensor_tensor(qk_dec[:, par, 0], q_raw[:, par], alpha[:, par], ALU.mult).then_inc(level0_set, 1)

            def decay(n, par, l):
                w = 2 ** (l - 1)
                m = N // (2 * w)
                src = spans if l > 1 else alpha
                off = (0 if l > 1 else par * N) + (0 if l < 3 else 2 * (N // 2 - N // 2 ** (l - 1)))
                pair = view(qk_dec, par * 2 * N + w, [[N - w, 2], [2 * w, m], [1, w]])
                other = view(src, off, [[1, 2], [2, m], [0, w]])
                dve.wait_ge(level_mm, LEVELS * n + l)
                dve.wait_ge(k_set, n + 1) if l == 1 else dve.wait_ge(span_set, 5 * n + l - 1)
                dve.wait_ge(level0_set, n + 1) if l == 1 else dve.wait_ge(decayed, OUTER * n + l - 1)
                nc.vector.tensor_tensor(pair, pair, other, ALU.mult).then_inc(decayed, 1)
                if l < LEVELS - 1:
                    to = 2 * (N // 2 - N // 2 ** l)
                    nc.vector.tensor_tensor(spans[:, to:to + m], view(src, off, [[2, m]]),
                                            view(src, off + 1, [[2, m]]), ALU.mult).then_inc(span_set, 1)

            def mask(n, half):
                slots = slice(0, 4) if half == 0 else slice(4, 6)
                of_bank = (bank_lo, bank_hi)[half][:, 0:(4 if half == 0 else 2) * N_IN]
                dve.wait_ge(level_mm, LEVELS * n + (3 if half == 0 else 5))
                nc.vector.tensor_tensor(by_level[:, slots].rearrange("p l b t -> p l (b t)"),
                                        of_bank.rearrange("p (l m) -> p l m", m=N_IN),
                                        owned[:, slots], ALU.mult).then_inc(masked, 1)
                if half == 1:
                    dve.wait_ge(masked, 2 * n + 2)
                    positive(dve, attnT_set, n)
                    nc.vector.tensor_reduce(blocks[:].rearrange("p b t -> p (b t)"),
                                            by_level[:].rearrange("p l b t -> p (b t) l"), AX,
                                            ALU.add).then_inc(blocks_set, 1)

            def squares_in(n):
                dve.wait_ge(norm_mm, n + 1)
                positive(dve, rnorm_set, n)
                nc.vector.tensor_scalar(norm_sq[:].rearrange("p a b -> p (a b)"), bank_k[:, 0:2 * GB],
                                        NORM_EPS * NORM_EPS, None, ALU.max).then_inc(norm_sq_set, 1)

            def v_scaled(n, par):
                dve.wait_ge(v_mm, n + 1)
                dve.wait_ge(rnorm_set, n + 1)
                if not (isinstance(n, int) and n < 2):
                    dve.wait_ge(o_mm, n - 1)
                nc.vector.tensor_tensor(v_sb[:, par], bank_gv[:].rearrange("p (b v) -> p b v", b=GB),
                                        rnorm[:, par, 1].unsqueeze(2).broadcast_to([P, GB, P]),
                                        ALU.mult).then_inc(v_set, 1)

            def o_scaled(n, par):
                dve.wait_ge(o_mm, n + 1)
                positive(dve, oT_mm, n)
                nc.vector.tensor_tensor(o_sb[:], bank_o[:].rearrange("p (b v) -> p b v", b=GB),
                                        rnorm[:, par, 0].unsqueeze(2).broadcast_to([P, GB, P]),
                                        ALU.mult).then_inc(o_set, 1)

            SMALL = 11
            def softmaxed_gate(i):
                base = SMALL * (i - 1)
                count = [0]

                def link(ins, plain=False):
                    ins.then_inc(small, 1)
                    count[0] += 1
                    (wait_first if plain else dve.wait_ge)(small, base + count[0])

                def wide(a):
                    return a.unsqueeze(2).broadcast_to([P, GB, E])

                dve.wait_ge(gate_exp_set, i)
                link(nc.vector.tensor_reduce(gate_sum[:], gate_exp[:], AX, ALU.add))
                link(nc.vector.reciprocal(gate_sum[:], gate_sum[:]))
                link(nc.vector.tensor_tensor(gate_exp[:], gate_exp[:], wide(gate_sum[:]), ALU.mult), True)
                for b in range(GB):
                    ins = nc.vector.max(top_val[:, b], gate_exp[:, b])
                link(ins, True)
                for b in range(GB):
                    ins = nc.vector.max_index(top_idx[:, b], top_val[:, b], gate_exp[:, b])
                link(ins)
                link(nc.vector.tensor_copy(top_num[:], top_idx[:]))
                every = experts[:].unsqueeze(1).broadcast_to([P, GB, E])
                nc.vector.tensor_tensor(is_first[:], every, top_num[:, :, 0:1].broadcast_to([P, GB, E]), ALU.is_equal)
                nc.vector.tensor_tensor(is_second[:], every, top_num[:, :, 1:2].broadcast_to([P, GB, E]), ALU.is_equal)
                link(nc.vector.tensor_tensor(top_sum[:], top_val[:, :, 0], top_val[:, :, 1], ALU.add))
                nc.vector.tensor_scalar(top_sum[:], top_sum[:], TOPW_EPS, None, ALU.add)
                link(nc.vector.tensor_tensor(is_first[:], is_first[:], is_second[:], ALU.add))
                nc.vector.reciprocal(top_sum[:], top_sum[:])
                link(nc.vector.tensor_tensor(weight[:], gate_exp[:], is_first[:], ALU.mult))
                link(nc.vector.tensor_tensor(weight[:], weight[:], wide(top_sum[:]), ALU.mult))
                pairs = weight[:].rearrange("p b (j e) -> p j b e", e=2)
                nc.vector.tensor_copy(weight_col[0:64], pairs[0:64, :, :, 0])
                link(nc.vector.tensor_copy(weight_col[64:P], pairs[64:P, :, :, 1]))
                assert count[0] == SMALL
                
            def tail_piece(i, s):
                if s == 0:
                    dve.wait_ge(x_res_set, i)
                    for f in (WO0, WO1):
                        dve.wait_ge(tail_mm[f], fills(i, f) + 1)
                        nc.vector.tensor_tensor(x_mid[:, 2 * f:2 * f + 2],
                                                tails[f][:].rearrange("p (b d) -> p b d", b=2),
                                                x_res[:, 2 * f:2 * f + 2], ALU.add).then_inc(tail_free[f], 1)
                    for f in (WO0, WO1):
                        dve.wait_ge(tail_free[f], fills(i, f) + 1)
                    layernorm(i, 1, x_mid)
                if s == 2:
                    dve.wait_ge(tail_mm[0], fills(i, SCORES) + 1)
                    nc.vector.tensor_reduce(prob_rsum[:], tail0[:].rearrange("p (b t) -> p b t", b=GB), AX,
                                            ALU.max).then_inc(row_stat, 1)
                    dve.wait_ge(row_stat, 2 * (i - 1) + 1)
                    nc.vector.tensor_scalar(neg_max[:], prob_rsum[:], -1.0, None, ALU.mult).then_inc(max_set, 1)
                if s == 4:
                    dve.wait_ge(tail_free[0], fills(i, SCORES) + 1)
                    nc.vector.reciprocal(prob_rsum[:], prob_sum[:]).then_inc(row_stat, 1)
                    dve.wait_ge(row_stat, 2 * (i - 1) + 2)
                    for f in (AV0, AV1):
                        dve.wait_ge(tail_mm[f % 2], fills(i, f) + 1)
                        for m in range(2):
                            b = 2 * (f - AV0) + m
                            ins = nc.vector.scalar_tensor_tensor(
                                out=x_mid[:, b], in0=tails[f % 2][:, D * m:D * m + D], scalar=prob_rsum[:, b:b + 1],
                                in1=x_mid[:, b], op0=ALU.mult, op1=ALU.add)
                        ins.then_inc(tail_free[f % 2], 1)
                    for f in (AV0, AV1):
                        dve.wait_ge(tail_free[f % 2], fills(i, f) + 1)
                    layernorm(i, 2, x_mid)
                if s == 5:
                    dve.wait_ge(tail_free[1], fills(i, X3T1) + 1)
                    nc.vector.tensor_reduce(pooled[:], xnT2[:].rearrange("p c (b t) -> p (c b) t", b=GB), AX,
                                            ALU.add).then_inc(pooled_set, 1)
                if s == 6:
                    dve.wait_ge(tail_mm[0], fills(i, GATE) + 1)
                    nc.vector.tensor_scalar(logits[:].rearrange("p b e -> p (b e)"), tail0[:, 0:GB * E], 1.0 / T, None,
                                            ALU.mult).then_inc(tail_free[0], 1)
                    dve.wait_ge(tail_free[0], fills(i, GATE) + 1)
                    nc.vector.tensor_reduce(gate_max[:], logits[:], AX, ALU.max).then_inc(gate_max_set, 1)
                    dve.wait_ge(gate_max_set, i)
                    nc.vector.tensor_tensor(logits[:], logits[:], gate_max[:].unsqueeze(2).broadcast_to([P, GB, E]),
                                            ALU.subtract).then_inc(logits_set, 1)
                if s == 7:
                    for j in range(EJ):
                        f = H0 + j
                        dve.wait_ge(tail_free[f % 2], fills(i, f) + 1)
                        ins = nc.vector.tensor_tensor(
                            hidden[:, j].rearrange("p (b t) -> p b t", b=GB),
                            hidden[:, j].rearrange("p (b t) -> p b t", b=GB),
                            weight_col[:, j].unsqueeze(2).broadcast_to([P, GB, T]), ALU.mult)
                    ins.then_inc(weighted, 1)

            def late_piece(i, s):
                if s == 6:
                    softmaxed_gate(i)
                if s == 7:
                    dve.wait_ge(tail_mm[1], fills(i, WT) + 1)
                    nc.vector.tensor_copy(weightT[:].rearrange("e b t -> e (b t)"), tail1[0:E, :]).then_inc(tail_free[1], 1)
                    dve.wait_ge(out_free, 16 * i)
                    for f in (UP0, UP1):
                        k = f - UP0
                        dve.wait_ge(tail_mm[k], fills(i, f) + 1)
                        nc.vector.tensor_tensor(out_sb[:, 2 * k:2 * k + 2],
                                                tails[k][:].rearrange("p (b d) -> p b d", b=2),
                                                x_mid[:, 2 * k:2 * k + 2], ALU.add).then_inc(tail_free[k], 1)

            def head_start(n, par):
                squares_in(n)
                v_scaled(n, par)

            def body(i, tail):
                dve.wait_ge(x_in, 16 * (i + 1))
                layernorm(i, 0, x_next)
                if tail:
                    tail_piece(i, 0)
                q_decayed(i * H, 0)
                head_start(i * H, 0)
                for h in range(H):
                    n, par = i * H + h, h % 2
                    decay(n, par, 1)
                    decay(n, par, 2)
                    if h > 0:
                        o_scaled(n - 1, 1 - par)
                    if tail and h > 0:
                        tail_piece(i, h)
                    decay(n, par, 3)
                    if h < H - 1:
                        q_decayed(n + 1, 1 - par)
                    decay(n, par, 4)
                    mask(n, 0)
                    decay(n, par, 5)
                    decay(n, par, 6)
                    mask(n, 1)
                    if h < H - 1:
                        head_start(n + 1, 1 - par)
                    if tail:
                        late_piece(i, h)
                o_scaled(i * H + H - 1, (H - 1) % 2)

            dve.wait_ge(c_in, N_C)
            body(0, False)
            with dve.Fori(1, NG) as i:
                body(i, True)
            for s in range(H):
                tail_piece(NG, s)
                late_piece(NG, s)

        @block.tensor
        def _(pe):
            mm = nc.tensor.matmul

            def project(w, dst, h):
                for c in range(KC):
                    last = mm(dst[:], w[:, c, P * h:P * h + P], xnT[:, c], start=(c == 0), stop=(c == KC - 1))
                return last

            def project_g(n, h):
                positive(pe, v_set, n)
                project(wg_sb, bank_gv, h).then_inc(g_mm, 1)

            def project_q(n, h):
                positive(pe, q_set, n)
                project(wq_sb, bank_q, h).then_inc(q_mm, 1)

            def project_k(n, h):
                positive(pe, norm_sq_set, n)
                project(wk_sb, bank_k, h).then_inc(k_mm, 1)

            def project_v(n, h):
                pe.wait_ge(alpha_set, n + 1)
                for b in range(GB):
                    for c in range(KC):
                        last = mm(bank_gv[:, P * b:P * b + P], xnT[:, c, T * b:T * b + T], wv_sb[:, c, P * h:P * h + P],
                                  start=(c == 0), stop=(c == KC - 1))
                last.then_inc(v_mm, 1)

            def norms(n):
                pe.wait_ge(q_set, n + 1)
                pe.wait_ge(k_set, n + 1)
                for a in range(2):
                    for b in range(GB):
                        last = mm(bank_k[:, GB * a + b:GB * a + b + 1], squares[:, a, T * b:T * b + T], ones[:, 0:1],
                                  start=True, stop=True)
                last.then_inc(norm_mm, 1)

            def block_products(dst, slot, left, right):
                for b in range(GB):
                    for r in range(T // BLOCK):
                        at = T * b + BLOCK * r
                        to = slot * GB * BLOCK + b * BLOCK
                        last = mm(dst[BLOCK * r:BLOCK * r + BLOCK, to:to + BLOCK], left[:, at:at + BLOCK],
                                  right[:, at:at + BLOCK], start=True, stop=True)
                return last

            def level(n, par, l):
                q, k = qk_dec[:, par, 0], qk_dec[:, par, 1]
                if l > 0:
                    pe.wait_ge(decayed, OUTER * n + l)
                if l == 0:
                    pe.wait_ge(level0_set, n + 1)
                    pe.wait_ge(k_set, n + 1)
                    pe.wait_ge(q_set, n + 1)
                    positive(pe, masked, 2 * n)
                    block_products(bank_lo, 0, k, q_raw[:, par])
                    last = block_products(bank_lo, 1, k, q)
                elif l < 3:
                    last = block_products(bank_lo, l + 1, k, q)
                elif l < INNER:
                    last = block_products(bank_hi, l - 3, k, q)
                else:
                    if l == INNER:
                        positive(pe, oT_set, n)
                    w = 2 ** l
                    for b in range(GB):
                        for s in range(0, T, 2 * w):
                            at = T * b + s
                            last = mm(bank_o[s:s + w, at + w:at + 2 * w], k[:, at:at + w], q[:, at + w:at + 2 * w],
                                      start=True, stop=True)
                last.then_inc(level_mm, 1)

            def attend(n, par):
                pe.wait_ge(attnT_set, n + 1)
                pe.wait_ge(v_set, n + 1)
                for b in range(GB):
                    last = mm(bank_o[:, P * b:P * b + P], attnT[:, b], v_sb[:, par, b], start=True, stop=True)
                last.then_inc(o_mm, 1)

            def attend_transposed(n):
                pe.wait_ge(o_set, n + 1)
                for b in range(GB):
                    last = nc.tensor.transpose(bank_o[:, P * b:P * b + P], o_sb[:, b], ident[:])
                last.then_inc(oT_mm, 1)

            def fill(i, f):
                positive(pe, tail_free[f % 2], fills(i, f))
                return tails[f % 2]

            def transposed(i, f0):
                for c in range(KC):
                    dst = fill(i, f0 + c)
                    for b in range(GB):
                        last = nc.tensor.transpose(dst[:, T * b:T * b + T], xn[:, b, P * c:P * c + P], ident[:])
                    last.then_inc(tail_mm[(f0 + c) % 2], 1)

            def pre(i, heads, tail):
                if tail:
                    pe.wait_ge(ctx_in, 16 * (KC + 1) * i)
                    pe.wait_ge(oT_set, H * i)
                    for f in (WO0, WO1):
                        dst = fill(i, f)
                        for m in range(2):
                            b = 2 * f + m
                            for h in range(H):
                                last = mm(dst[:, D * m:D * m + D], oT_sb[:, h, T * b:T * b + T], wo_sb[:, h],
                                          start=(h == 0), stop=(h == H - 1))
                        last.then_inc(tail_mm[f], 1)
                    for f in (PROJ0, PROJ1):
                        j = f - PROJ0
                        dst = fill(i, f)
                        for c in range(KC):
                            last = mm(dst[:], xw_sb[:, c, P * j:P * j + P], ctxT_sb[:, c].rearrange("p b t -> p (b t)"),
                                      start=(c == 0), stop=(c == KC - 1))
                        last.then_inc(tail_mm[j], 1)
                if heads:
                    pe.wait_ge(ln_out, norms_done(i, 0) + 1)
                    transposed(i, XT0)
                    pe.wait_ge(tail_free[1], fills(i, XT1) + 1)
                    pe.wait_ge(tail_free[0], fills(i, XT0) + 1)

            def tail_piece(i, s):
                if s == 0:
                    pe.wait_ge(ln_out, norms_done(i, 1) + 1)
                    transposed(i, X2T0)
                if s == 1:
                    pe.wait_ge(tail_free[0], fills(i, X2T0) + 1)
                    pe.wait_ge(tail_free[1], fills(i, X2T1) + 1)
                    dst = fill(i, SCORES)
                    for b in range(GB):
                        for c in range(KC):
                            last = mm(dst[:, T * b:T * b + T], xnT2[:, c, T * b:T * b + T], projT[:, c, b],
                                      start=(c == 0), stop=(c == KC - 1))
                    last.then_inc(tail_mm[0], 1)
                if s == 2:
                    pe.wait_ge(tail_free[0], fills(i, SCORES) + 1)
                    dst = fill(i, PT)
                    for b in range(GB):
                        last = nc.tensor.transpose(dst[:, T * b:T * b + T], probs[:, b], ident[:])
                    last.then_inc(tail_mm[1], 1)
                if s == 3:
                    pe.wait_ge(tail_free[1], fills(i, PT) + 1)
                    for f in (AV0, AV1):
                        dst = fill(i, f)
                        for m in range(2):
                            b = 2 * (f - AV0) + m
                            last = mm(dst[:, D * m:D * m + D], probsT[:, b], ctx_sb[:, b], start=True, stop=True)
                        last.then_inc(tail_mm[f % 2], 1)
                if s == 4:
                    pe.wait_ge(ln_out, norms_done(i, 2) + 1)
                    transposed(i, X3T0)
                if s == 5:
                    pe.wait_ge(pooled_set, i)
                    dst = fill(i, GATE)
                    for b in range(GB):
                        for c in range(KC):
                            last = mm(dst[:, E * b:E * b + E],
                                      pooled[:, GB * c + b:GB * c + b + 1].broadcast_to([P, P]), gate_sb[:, c],
                                      start=(c == 0), stop=(c == KC - 1))
                    last.then_inc(tail_mm[0], 1)
                if s == 5 or s == 6:
                    for f in (H0,) if s == 5 else (H1, H2, H3):
                        j = f - H0
                        dst = fill(i, f)
                        for c in range(KC):
                            last = mm(dst[:], down_sb[:, c, P * j:P * j + P], xnT2[:, c], start=(c == 0),
                                      stop=(c == KC - 1))
                        last.then_inc(tail_mm[f % 2], 1)
                if s == 7:
                    pe.wait_ge(small, 11 * i)
                    dst = fill(i, WT)
                    for b in range(GB):
                        last = nc.tensor.transpose(dst[0:E, T * b:T * b + T], weight[:, b], ident[:])
                    last.then_inc(tail_mm[1], 1)
                    pe.wait_ge(weighted, i)
                    pe.wait_ge(tail_free[1], fills(i, WT) + 1)
                    for f in (UP0, UP1):
                        dst = fill(i, f)
                        for m in range(2):
                            b = 2 * (f - UP0) + m
                            for j in range(EJ):
                                mm(dst[:, D * m:D * m + D], hidden[:, j, T * b:T * b + T], up_sb[:, j],
                                   start=(j == 0), stop=False)
                            last = mm(dst[:, D * m:D * m + D], weightT[:, b], upb_sb[:], start=False, stop=True)
                        last.then_inc(tail_mm[f % 2], 1)

            def body(i, tail):
                pre(i, True, tail)
                n = i * H
                project_g(n, 0)
                project_q(n, 0)
                project_k(n, 0)
                project_v(n, 0)
                norms(n)
                for h in range(H):
                    n, par, more = i * H + h, h % 2, h < H - 1
                    if more:
                        project_g(n + 1, h + 1)
                    level(n, par, 0)
                    if more:
                        project_q(n + 1, h + 1)
                    level(n, par, 1)
                    if h > 0:
                        attend(n - 1, 1 - par)
                    if more:
                        project_k(n + 1, h + 1)
                    level(n, par, 2)
                    if h > 0:
                        attend_transposed(n - 1)
                    level(n, par, 3)
                    if more:
                        project_v(n + 1, h + 1)
                    level(n, par, 4)
                    if more:
                        norms(n + 1)
                    level(n, par, 5)
                    level(n, par, 6)
                    if tail:
                        tail_piece(i, h)
                attend(n, par)
                attend_transposed(n)

            pe.wait_ge(c_in, N_C)
            pe.wait_ge(consts_set, 1)
            pe.wait_ge(w_in, N_W)
            body(0, False)
            with pe.Fori(1, NG) as i:
                body(i, True)
            pre(NG, False, True)
            for s in range(H):
                tail_piece(NG, s)


def kernel(x, ctx_1024, L0_attn_Wq, L0_attn_Wk, L0_attn_Wv, L0_attn_Wg, L0_attn_Wo, L0_xattn_W,
           L0_ffn_gate_w, L0_ffn_down_w, L0_ffn_down_b, L0_ffn_up_w, L0_ffn_up_b):
    import concourse.bacc as bacc
    from concourse.bass_utils import run_bass_kernel_spmd

    E, BN, D = L0_ffn_down_w.shape
    ident, owned, experts = shape_constants(4)
    arrays = {
        "x": x,
        "ctx": ctx_1024,
        "ctxT": np.transpose(ctx_1024, (0, 2, 1)),
        "wq": L0_attn_Wq, "wk": L0_attn_Wk, "wv": L0_attn_Wv, "wg": L0_attn_Wg, "wo": L0_attn_Wo,
        "xwT": np.transpose(L0_xattn_W),
        "gateT": np.transpose(L0_ffn_gate_w),
        "downT": np.transpose(np.reshape(L0_ffn_down_w, (E * BN, D))),
        "down_b": np.transpose(np.reshape(L0_ffn_down_b, (E * BN // P, P))),
        "up": np.reshape(np.transpose(L0_ffn_up_w, (0, 2, 1)), (E * BN, D)),
        "up_b": L0_ffn_up_b,
        "ident_c": ident, "owned_c": owned, "experts_c": experts,
    }
    arrays = {name + "_dram": np.ascontiguousarray(a) for name, a in arrays.items()}
    nc = bacc.Bacc("TRN2", target_bir_lowering=False, num_devices=1)
    args = [nc.dram_tensor(name, a.shape, mybir.dt.from_np(a.dtype), kind="ExternalInput").ap()
            for name, a in arrays.items()]
    out = nc.dram_tensor("out_dram", x.shape, F32, kind="ExternalOutput").ap()
    decoder_kernel(nc, *args, out)
    r = run_bass_kernel_spmd(nc, [arrays], core_ids=[0])
    return r.results[0]["out_dram"]
```

```python
from contextlib import ExitStack

import numpy as np

import concourse.bass as bass
from concourse import mybir

P = 128
F32 = mybir.dt.float32
F32R = mybir.dt.float32r
I32 = mybir.dt.int32
U32 = mybir.dt.uint32
ALU = mybir.AluOpType
ACT = mybir.ActivationFunctionType
AX = mybir.AxisListType.X

LN_EPS = 1e-5
NORM_EPS = 1e-12
TOPW_EPS = 1e-8
LEVELS = 7
BLOCK = 32
OUTER = LEVELS - 1
INNER = 5


def shape_constants(sequences):
    ident = np.eye(P, dtype=np.float32)
    s = np.arange(P)[:, None] % BLOCK
    t = np.arange(BLOCK)[None, :]
    owned = [s == t] + [((s >> (l + 1)) == (t >> (l + 1))) & ((s >> l) % 2 == 0) & ((t >> l) % 2 == 1)
                        for l in range(INNER)]
    owned = np.stack([np.tile(m, (1, sequences)) for m in owned], axis=1).astype(np.float32)
    experts = np.broadcast_to(np.arange(8, dtype=np.float32), (P, 8)).copy()
    return ident, owned, experts


def decoder_kernel(nc, x, ctx, ctxT, wq, wk, wv, wg, wo, xwT, gateT, downT, down_b, up, up_b,
                   ident_c, owned_c, experts_c, out):
    B, T, D = x.shape
    H = wq.shape[1] // P
    KC = D // P
    GB = 4
    NG = B // GB
    N = GB * T
    E = gateT.shape[1]
    EJ = downT.shape[1] // P
    assert T == P and D == 256 and N == 512 and E == 8

    with ExitStack() as stack:
        def sb(name, shape, dt=F32):
            return stack.enter_context(nc.sbuf_tensor(name, shape, dt))

        def bank(name):
            return stack.enter_context(nc.psum_tensor(name, [P, 512], F32))

        def sem(name):
            return stack.enter_context(nc.semaphore(name))

        HI, LO = 0, 1
        wq_sb, wk_sb, wv_sb, wg_sb = (
            sb(n, [P, 2, KC, H * P], F32R) for n in ("wq_sb", "wk_sb", "wv_sb", "wg_sb"))
        wo_sb = sb("wo_sb", [P, H, D])
        xw_sb = sb("xw_sb", [P, KC, D])
        gate_sb = sb("gate_sb", [P, KC, E])
        down_sb = sb("down_sb", [P, KC, EJ * P])
        downb_sb = sb("downb_sb", [P, EJ])
        up_sb = sb("up_sb", [P, EJ, D])
        upb_sb = sb("upb_sb", [E, D])
        ident = sb("ident", [P, P])
        N_IN = GB * BLOCK
        owned = sb("owned", [P, 1 + INNER, N_IN])
        experts = sb("experts", [P, E])
        ones = sb("ones", [P, 2])
        scratch = sb("scratch", [P, 1])
        pool_scratch = sb("pool_scratch", [P, 1])
        neg_half = sb("neg_half", [P, 8])
        x_next = sb("x_next", [P, GB, D])
        x_res = sb("x_res", [P, GB, D])
        ctx_sb = sb("ctx_sb", [P, GB, D])
        ctxT_sb = sb("ctxT_sb", [P, KC, GB, T])
        stats = sb("stats", [P, GB, 6])
        mean_var = sb("mean_var", [P, GB, 2])
        var_eps = sb("var_eps", [P, GB])
        rstd = sb("rstd", [P, GB])
        xn = sb("xn", [P, GB, D])
        xnT = sb("xnT", [P, 2, KC, N], F32R)
        alpha = sb("alpha", [P, 2, N])
        q_raw = sb("q_raw", [P, 2, N])
        qk_dec = sb("qk_dec", [P, 2, 2, N])
        self_diag = sb("self_diag", [P, 2 * GB, BLOCK])
        spans = sb("spans", [P, N])
        self_sq = sb("self_sq", [P, 2 * GB])
        norm_sq = sb("norm_sq", [P, 2, GB])
        rnorm = sb("rnorm", [P, 2, 2, GB])
        v_raw = sb("v_raw", [P, 2, GB, 2, P])
        v_sb = sb("v_sb", [P, 2, GB, P])
        by_level = sb("by_level", [P, 1 + INNER, GB, BLOCK])
        blocks = sb("blocks", [P, GB, BLOCK])
        attnT = sb("attnT", [P, GB, T])
        o_sb = sb("o_sb", [P, GB, P])
        oT_sb = sb("oT_sb", [P, H, N])
        x_mid = sb("x_mid", [P, GB, D])
        xnT2 = sb("xnT2", [P, KC, N])
        projT = sb("projT", [P, KC, GB, T])
        row_max = sb("row_max", [P, GB])
        neg_max = sb("neg_max", [P, GB])
        probs = sb("probs", [P, GB, T])
        prob_sum = sb("prob_sum", [P, GB])
        prob_rsum = sb("prob_rsum", [P, GB])
        probsT = sb("probsT", [P, GB, T])
        pooled = sb("pooled", [P, KC * GB])
        logits = sb("logits", [P, GB, E])
        gate_max = sb("gate_max", [P, GB])
        gate_exp = sb("gate_exp", [P, GB, E])
        gate_sum = sb("gate_sum", [P, GB])
        top_val = sb("top_val", [P, GB, 8])
        top_idx = sb("top_idx", [P, GB, 8], U32)
        top_num = sb("top_num", [P, GB, 8])
        is_first = sb("is_first", [P, GB, E])
        is_second = sb("is_second", [P, GB, E])
        top_sum = sb("top_sum", [P, GB])
        weight = sb("weight", [P, GB, E])
        weight_col = sb("weight_col", [P, EJ, GB])
        weightT = sb("weightT", [E, GB, T])
        hidden = sb("hidden", [P, EJ, N])
        out_sb = sb("out_sb", [P, GB, D])

        stage_g = hidden[:, 0:EJ].rearrange("p j n -> p (j n)")
        stage_q = oT_sb[:, 0:4].rearrange("p h n -> p (h n)")
        stage_k = oT_sb[:, 4:8].rearrange("p h n -> p (h n)")
        stage_v = v_raw[:].rearrange("p r b h v -> p (r b h v)")
        staged = ((wg_sb, stage_g), (wq_sb, stage_q), (wk_sb, stage_k), (wv_sb, stage_v))

        bank_q, bank_k, bank_gv, bank_lo, bank_hi, bank_o, tail0, tail1 = (
            bank(n) for n in ("bank_q", "bank_k", "bank_gv", "bank_lo", "bank_hi", "bank_o", "tail0", "tail1"))
        tails = (tail0, tail1)

        w_hi, w_split, xT_hi = sem("w_hi"), sem("w_split"), sem("xT_hi")
        wg_in, wq_in, wk_in, wv_in = (sem(n) for n in ("wg_in", "wq_in", "wk_in", "wv_in"))
        w_in, c_in, x_in, ctx_in, ctxT_in, out_free = (
            sem(n) for n in ("w_in", "c_in", "x_in", "ctx_in", "ctxT_in", "out_free"))
        consts_set = sem("consts_set")
        g_mm, q_mm, k_mm, v_mm, norm_mm, level_mm, o_mm, oT_mm = (
            sem(n) for n in ("g_mm", "q_mm", "k_mm", "v_mm", "norm_mm", "level_mm", "o_mm", "oT_mm"))
        tail_mm = (sem("tail_mm0"), sem("tail_mm1"))
        tail_free = (sem("tail_free0"), sem("tail_free1"))
        alpha_set, q_set, k_set, oT_set, attnT_set = (
            sem(n) for n in ("alpha_set", "q_set", "k_set", "oT_set", "attnT_set"))
        gate_exp_set = sem("gate_exp_set")
        self_set, v_raw_set = sem("self_set"), sem("v_raw_set")
        level0_set, decayed, span_set, masked, blocks_set, norm_sq_set, v_set, o_set = (
            sem(n) for n in ("level0_set", "decayed", "span_set", "masked", "blocks_set", "norm_sq_set", "v_set", "o_set"))
        ln_stat, ln_var, ln_out = sem("ln_stat"), sem("ln_var"), sem("ln_out")
        ln_rstd, rnorm_set, x_res_set = sem("ln_rstd"), sem("rnorm_set"), sem("x_res_set")
        row_stat, max_set, pooled_set, gate_max_set, logits_set, small, weighted = (
            sem(n) for n in ("row_stat", "max_set", "pooled_set", "gate_max_set", "logits_set", "small", "weighted"))

        (XT0, XT1, WO0, WO1, X2T0, X2T1, SCORES, PT, AV0, AV1, X3T0, X3T1,
         GATE, H0, H1, H2, H3, WT, UP0, UP1, KEY0, KEY1) = range(22)

        def fills(i, f):
            if isinstance(i, int) and i == 0:
                return 0 if f <= XT1 else 1
            return 11 * i - 9 + f // 2 - (1 if isinstance(i, int) and i == NG else 0)

        def norms_done(i, k):
            if isinstance(i, int) and i == 0:
                return 0
            return 3 * i - 2 + k - (1 if isinstance(i, int) and i == NG else 0)

        def positive(engine, s, value):
            if not isinstance(value, int) or value > 0:
                engine.wait_ge(s, value)

        def view(tensor, start, dims):
            whole = tensor[:]
            return bass.AP(whole.tensor, whole.offset + start, [list(whole.ap[0])] + dims)

        N_W, N_C = 16 * 7, 16 * 3

        block = stack.enter_context(nc.Block())

        @block.sync
        def _(sp):
            def load_x(i):
                sp.dma_start(x_next[:], x[bass.ts(i, GB)].rearrange("b t d -> t b d")).then_inc(x_in, 16)

            def load_ctxT(i):
                for c in range(KC):
                    sp.dma_start(ctxT_sb[:, c], ctxT[bass.ts(i, GB), P * c:P * c + P].rearrange("b p t -> p b t")
                                 ).then_inc(ctxT_in, 16)

            def load_ctx(i):
                sp.dma_start(ctx_sb[:], ctx[bass.ts(i, GB)].rearrange("b t d -> t b d")).then_inc(ctx_in, 16)

            load_x(0)
            for dst, src in ((ident, ident_c), (owned, owned_c), (experts, experts_c)):
                sp.dma_start(dst[:], src).then_inc(c_in, 16)
            for dst, src, s in ((stage_g, wg, wg_in), (stage_q, wq, wq_in), (stage_k, wk, wk_in), (stage_v, wv, wv_in)):
                sp.dma_start(dst.rearrange("p (c n) -> p c n", c=KC), src.rearrange("(c p) n -> p c n", p=P)).then_inc(s, 16)
            load_ctxT(0)
            load_ctx(0)
            sp.dma_start(wo_sb[:], wo.rearrange("(h p) n -> p h n", p=P)).then_inc(w_in, 16)
            for dst, src in ((xw_sb, xwT), (gate_sb, gateT), (down_sb, downT)):
                sp.dma_start(dst[:], src.rearrange("(c p) n -> p c n", p=P)).then_inc(w_in, 16)
            sp.dma_start(downb_sb[:], down_b).then_inc(w_in, 16)
            sp.dma_start(up_sb[:], up.rearrange("(j p) n -> p j n", p=P)).then_inc(w_in, 16)
            sp.dma_start(upb_sb[:], up_b).then_inc(w_in, 16)
            sp.wait_ge(ln_out, 1)
            sp.wait_ge(x_res_set, 1)
            load_x(1)

            def store(i):
                for f in (UP0, UP1):
                    sp.wait_ge(tail_free[f % 2], fills(i, f) + 1)
                sp.dma_start(out[bass.ts(i - 1, GB)].rearrange("b t d -> t b d"), out_sb[:]).then_inc(out_free, 16)

            def body(i, last):
                sp.wait_ge(tail_mm[1], fills(i, XT1))
                load_ctxT(i)
                if not last:
                    sp.wait_ge(x_res_set, i + 1)
                    sp.wait_ge(ln_out, norms_done(i, 0) + 1)
                    load_x(i + 1)
                sp.wait_ge(tail_mm[1], fills(i, AV1) + 1)
                load_ctx(i)
                store(i)

            with sp.Fori(1, NG - 1) as i:
                body(i, False)
            body(NG - 1, True)
            store(NG)
            sp.wait_ge(out_free, 16 * (NG + 1))

        @block.gpsimd
        def _(pool):
            nc.gpsimd.memset(neg_half[:], -0.5)
            nc.gpsimd.memset(ones[:], 1.0)
            nc.gpsimd.memset(out_sb[:], 0.0).then_inc(out_free, 16)
            nc.gpsimd.memset(attnT[:], 0.0).then_inc(consts_set, 1)
            pool.wait_ge(consts_set, 1)

            def ln_power(i, k):
                pool.wait_ge(ln_var, norms_done(i, k) + 1)
                positive(pool, ln_out, norms_done(i, k))
                nc.gpsimd.tensor_tensor(rstd[:], var_eps[:], neg_half[:, 0:GB], ALU.pow).then_inc(ln_rstd, 1)

            def keep_x(i):
                pool.wait_ge(x_in, 16 * (i + 1))
                if not (isinstance(i, int) and i == 0):
                    for f in (WO0, WO1):
                        pool.wait_ge(tail_free[f % 2], fills(i, f) + 1)
                nc.gpsimd.tensor_tensor(pool_scratch[:], neg_half[:, 0:1], neg_half[:, 0:1], ALU.mult)
                nc.gpsimd.tensor_copy(x_res[:], x_next[:]).then_inc(x_res_set, 1)

            def reciprocal_norms(n, par):
                pool.wait_ge(norm_sq_set, n + 1)
                if not (isinstance(n, int) and n < 2):
                    pool.wait_ge(v_set, n - 1)
                    pool.wait_ge(o_set, n - 1)
                nc.gpsimd.tensor_tensor(rnorm[:, par].rearrange("p a b -> p (a b)"),
                                        norm_sq[:].rearrange("p a b -> p (a b)"), neg_half[:],
                                        ALU.pow).then_inc(rnorm_set, 1)

            def q_decayed(n, par):
                pool.wait_ge(q_set, n + 1)
                pool.wait_ge(alpha_set, n + 1)
                if not (isinstance(n, int) and n < 2):
                    pool.wait_ge(level_mm, LEVELS * (n - 1))
                nc.gpsimd.tensor_tensor(qk_dec[:, par, 0], q_raw[:, par], alpha[:, par], ALU.mult).then_inc(level0_set, 1)

            def v_scaled(i, h):
                n, par = i * H + h, h % 2
                pool.wait_ge(v_raw_set, i * H + h // 2 * 2 + 2)
                pool.wait_ge(rnorm_set, n + 1)
                if not (isinstance(n, int) and n < 2):
                    pool.wait_ge(o_mm, n - 1)
                nc.gpsimd.tensor_tensor(v_sb[:, par], v_raw[:, h // 2 % 2, :, par],
                                        rnorm[:, par, 1].unsqueeze(2).broadcast_to([P, GB, P]),
                                        ALU.mult).then_inc(v_set, 1)

            def body(i, tail):
                ln_power(i, 0)
                q_decayed(i * H, 0)
                reciprocal_norms(i * H, 0)
                v_scaled(i, 0)
                keep_x(i)
                for h in range(H):
                    if tail and h == 0:
                        ln_power(i, 1)
                    if tail and h == 3:
                        ln_power(i, 2)
                    if h < H - 1:
                        q_decayed(i * H + h + 1, (h + 1) % 2)
                        reciprocal_norms(i * H + h + 1, (h + 1) % 2)
                        v_scaled(i, h + 1)

            body(0, False)
            with pool.Fori(1, NG) as i:
                body(i, True)
            ln_power(NG, 1)
            ln_power(NG, 2)

        @block.scalar
        def _(act):
            def head_in(n, par):
                act.wait_ge(g_mm, n + 1)
                if not (isinstance(n, int) and n < 2):
                    act.wait_ge(level_mm, LEVELS * (n - 1))
                nc.scalar.activation(alpha[:, par], bank_gv[:], ACT.Sigmoid).then_inc(alpha_set, 1)
                act.wait_ge(q_mm, n + 1)
                nc.scalar.copy(q_raw[:, par], bank_q[:]).then_inc(q_set, 1)
                act.wait_ge(k_mm, n + 1)
                nc.scalar.copy(qk_dec[:, par, 1], bank_k[:]).then_inc(k_set, 1)

            def v_out(i, m):
                pair, half = m // 2, m % 2
                act.wait_ge(v_mm, i * H + m + 1)
                positive(act, v_set, i * H + 2 * pair - 2)
                nc.scalar.copy(v_raw[:, pair % 2, 2 * half:2 * half + 2],
                               bank_gv[:].rearrange("p (b h v) -> p b h v", b=2, h=2)).then_inc(v_raw_set, 1)

            def oT_out(n, h):
                act.wait_ge(oT_mm, n + 1)
                nc.scalar.copy(oT_sb[:, h], bank_o[:]).then_inc(oT_set, 1)

            def expand(n):
                positive(act, o_mm, n)
                act.wait_ge(level_mm, LEVELS * (n + 1))
                near = bank_q[:, 0:GB * BLOCK].rearrange("p (b t) -> p b t", b=GB)
                far = bank_q[:, GB * BLOCK:3 * GB * BLOCK].rearrange("p (b t) -> p b t", b=GB)
                for lo in (0, 2 * BLOCK):
                    nc.scalar.copy(attnT[lo:lo + BLOCK, :, lo + BLOCK:lo + 2 * BLOCK], near[lo:lo + BLOCK])
                nc.scalar.copy(attnT[0:T // 2, :, T // 2:T], far[0:T // 2])
                act.wait_ge(blocks_set, n + 1)
                for r in range(T // BLOCK):
                    lo = BLOCK * r
                    last = nc.scalar.copy(attnT[lo:lo + BLOCK, :, lo:lo + BLOCK], blocks[lo:lo + BLOCK])
                last.then_inc(attnT_set, 1)

            def tail_to(dst, i, f):
                act.wait_ge(tail_mm[f % 2], fills(i, f) + 1)
                nc.scalar.copy(dst, tails[f % 2][:]).then_inc(tail_free[f % 2], 1)

            def gelu(i, f):
                j = f - H0
                act.wait_ge(tail_mm[f % 2], fills(i, f) + 1)
                nc.scalar.activation(hidden[:, j], tails[f % 2][:], ACT.Gelu,
                                     bias=downb_sb[:, j:j + 1]).then_inc(tail_free[f % 2], 1)

            def tail_first(i, s):
                if s == 1:
                    tail_to(xnT2[:, 0], i, X2T0)
                    tail_to(xnT2[:, 1], i, X2T1)
                if s == 2:
                    tail_to(probsT[:].rearrange("p b t -> p (b t)"), i, PT)
                if s == 4:
                    tail_to(xnT2[:, 0], i, X3T0)
                    tail_to(xnT2[:, 1], i, X3T1)
                if s == 6:
                    gelu(i, H3)

            def tail_middle(i, s):
                if s == 1:
                    act.wait_ge(max_set, i)
                    for b in range(GB):
                        last = nc.scalar.activation(probs[:, b], tail0[:, T * b:T * b + T], ACT.Exp,
                                                    bias=neg_max[:, b:b + 1], accum_out=prob_sum[:, b:b + 1])
                    last.then_inc(tail_free[0], 1)
                if s == 5:
                    act.wait_ge(logits_set, i)
                    nc.scalar.activation(gate_exp[:], logits[:], ACT.Exp).then_inc(gate_exp_set, 1)
                    gelu(i, H0)

            def tail_last(i, s):
                if s == 5:
                    gelu(i, H1)
                    gelu(i, H2)

            def split_weights(k):
                act.wait_ge((wg_in, wq_in, wk_in, wv_in)[k], 16)
                parts, whole = staged[k]
                nc.scalar.copy(parts[:, HI].rearrange("p c n -> p (c n)"), whole).then_inc(w_hi, 1)

            def body(i, tail, first=False):
                if first:
                    split_weights(0)
                for c in range(KC):
                    act.wait_ge(tail_mm[c], fills(i, XT0 + c) + 1)
                    nc.scalar.copy(xnT[:, HI, c], tails[c][:]).then_inc(xT_hi, 1)
                if first:
                    for k in range(1, 4):
                        split_weights(k)
                head_in(i * H, 0)
                v_out(i, 0)
                v_out(i, 1)
                if tail:
                    oT_out(i * H - 1, H - 1)
                for h in range(H):
                    n = i * H + h
                    if tail:
                        tail_first(i, h)
                    if h < H - 1:
                        head_in(n + 1, (h + 1) % 2)
                    if tail:
                        tail_middle(i, h)
                    if h + 2 < H:
                        v_out(i, h + 2)
                    expand(n)
                    if h > 0:
                        oT_out(n - 1, h - 1)
                    if tail:
                        tail_last(i, h)
                for c in range(KC):
                    tail_to(projT[:, c].rearrange("p b t -> p (b t)"), i, KEY0 + c)

            act.wait_ge(consts_set, 1)
            body(0, False, first=True)
            act.wait_ge(w_in, N_W)
            with act.Fori(1, NG) as i:
                body(i, True)
            oT_out(NG * H - 1, H - 1)
            for s in range(H):
                tail_first(NG, s)
                tail_middle(NG, s)
                tail_last(NG, s)

        @block.vector
        def _(dve):
            def wait_first(s, value):
                dve.wait_ge(s, value)
                nc.vector.memset(scratch[:], 0.0)

            def ln_stats(i, k, src):
                for b in range(GB):
                    last = nc.vector.bn_stats(stats[:, b], src[:, b])
                last.then_inc(ln_stat, 1)

            def ln_variance(i, k):
                base = norms_done(i, k)
                wait_first(ln_stat, 2 * base + 1)
                for b in range(GB):
                    last = nc.vector.bn_aggr(mean_var[:, b], stats[:, b])
                last.then_inc(ln_stat, 1)
                dve.wait_ge(ln_stat, 2 * base + 2)
                nc.vector.tensor_scalar(var_eps[:], mean_var[:, :, 1], LN_EPS, None, ALU.add).then_inc(ln_var, 1)

            def ln_normalize(i, k, src):
                dve.wait_ge(ln_rstd, norms_done(i, k) + 1)
                if k > 0:
                    f = (None, XT1, X2T1)[k]
                    if not (isinstance(i, int) and i == NG and k == 1):
                        dve.wait_ge(tail_mm[1], fills(i, f) + 1)
                for b in range(GB):
                    last = nc.vector.tensor_scalar(xn[:, b], src[:, b], mean_var[:, b, 0:1], rstd[:, b:b + 1],
                                                   ALU.subtract, ALU.mult)
                last.then_inc(ln_out, 1)

            def decay(n, par, l):
                w = 2 ** (l - 1)
                m = N // (2 * w)
                src = spans if l > 1 else alpha
                off = (0 if l > 1 else par * N) + (0 if l < 3 else 2 * (N // 2 - N // 2 ** (l - 1)))
                pair = view(qk_dec, par * 2 * N + w, [[N - w, 2], [2 * w, m], [1, w]])
                other = view(src, off, [[1, 2], [2, m], [0, w]])
                dve.wait_ge(level_mm, LEVELS * n + l)
                dve.wait_ge(k_set, n + 1) if l == 1 else dve.wait_ge(span_set, 5 * n + l - 1)
                dve.wait_ge(level0_set, n + 1) if l == 1 else dve.wait_ge(decayed, OUTER * n + l - 1)
                nc.vector.tensor_tensor(pair, pair, other, ALU.mult).then_inc(decayed, 1)
                if l < LEVELS - 1:
                    to = 2 * (N // 2 - N // 2 ** l)
                    nc.vector.tensor_tensor(spans[:, to:to + m], view(src, off, [[2, m]]),
                                            view(src, off + 1, [[2, m]]), ALU.mult).then_inc(span_set, 1)

            def mask(n, half):
                slots = slice(0, 4) if half == 0 else slice(4, 6)
                of_bank = (bank_lo, bank_hi)[half][:, 0:(4 if half == 0 else 2) * N_IN]
                dve.wait_ge(level_mm, LEVELS * n + (3 if half == 0 else 5))
                nc.vector.tensor_tensor(by_level[:, slots].rearrange("p l b t -> p l (b t)"),
                                        of_bank.rearrange("p (l m) -> p l m", m=N_IN),
                                        owned[:, slots], ALU.mult).then_inc(masked, 1)
                if half == 1:
                    dve.wait_ge(masked, 2 * n + 2)
                    positive(dve, attnT_set, n)
                    nc.vector.tensor_reduce(blocks[:].rearrange("p b t -> p (b t)"),
                                            by_level[:].rearrange("p l b t -> p (b t) l"), AX,
                                            ALU.add).then_inc(blocks_set, 1)

            def squares_in(n):
                dve.wait_ge(norm_mm, n + 1)
                positive(dve, rnorm_set, n)
                nc.vector.tensor_tensor(self_diag[:].rearrange("p (a b) t -> p a (b t)", a=2),
                                        bank_k[:, 0:2 * N_IN].rearrange("p (a m) -> p a m", a=2),
                                        owned[:, 0:1].broadcast_to([P, 2, N_IN]), ALU.mult).then_inc(self_set, 1)
                dve.wait_ge(self_set, 2 * n + 1)
                nc.vector.tensor_reduce(self_sq[:], self_diag[:], AX, ALU.add).then_inc(self_set, 1)
                dve.wait_ge(self_set, 2 * n + 2)
                nc.vector.tensor_scalar(norm_sq[:].rearrange("p a b -> p (a b)"), self_sq[:],
                                        NORM_EPS * NORM_EPS, None, ALU.max).then_inc(norm_sq_set, 1)

            def o_scaled(n, par):
                dve.wait_ge(o_mm, n + 1)
                positive(dve, oT_mm, n)
                nc.vector.tensor_tensor(o_sb[:], bank_o[:].rearrange("p (b v) -> p b v", b=GB),
                                        rnorm[:, par, 0].unsqueeze(2).broadcast_to([P, GB, P]),
                                        ALU.mult).then_inc(o_set, 1)

            SMALL = 11

            def softmaxed_gate(i, part):
                count = [SMALL * (i - 1) + (0, 5, 9)[part]]

                def link(ins, plain=False):
                    ins.then_inc(small, 1)
                    count[0] = count[0] + 1
                    (wait_first if plain else dve.wait_ge)(small, count[0])

                def wide(a):
                    return a.unsqueeze(2).broadcast_to([P, GB, E])

                if part == 0:
                    dve.wait_ge(gate_exp_set, i)
                    link(nc.vector.tensor_reduce(gate_sum[:], gate_exp[:], AX, ALU.add))
                    link(nc.vector.reciprocal(gate_sum[:], gate_sum[:]))
                    link(nc.vector.tensor_tensor(gate_exp[:], gate_exp[:], wide(gate_sum[:]), ALU.mult), True)
                    for b in range(GB):
                        ins = nc.vector.max(top_val[:, b], gate_exp[:, b])
                    link(ins, True)
                    for b in range(GB):
                        ins = nc.vector.max_index(top_idx[:, b], top_val[:, b], gate_exp[:, b])
                    link(ins)
                if part == 1:
                    link(nc.vector.tensor_copy(top_num[:], top_idx[:]))
                    every = experts[:].unsqueeze(1).broadcast_to([P, GB, E])
                    nc.vector.tensor_tensor(is_first[:], every, top_num[:, :, 0:1].broadcast_to([P, GB, E]),
                                            ALU.is_equal)
                    nc.vector.tensor_tensor(is_second[:], every, top_num[:, :, 1:2].broadcast_to([P, GB, E]),
                                            ALU.is_equal)
                    link(nc.vector.tensor_tensor(top_sum[:], top_val[:, :, 0], top_val[:, :, 1], ALU.add))
                    nc.vector.tensor_scalar(top_sum[:], top_sum[:], TOPW_EPS, None, ALU.add)
                    link(nc.vector.tensor_tensor(is_first[:], is_first[:], is_second[:], ALU.add))
                    nc.vector.reciprocal(top_sum[:], top_sum[:])
                    link(nc.vector.tensor_tensor(weight[:], gate_exp[:], is_first[:], ALU.mult))
                if part == 2:
                    link(nc.vector.tensor_tensor(weight[:], weight[:], wide(top_sum[:]), ALU.mult))
                    pairs = weight[:].rearrange("p b (j e) -> p j b e", e=2)
                    nc.vector.tensor_copy(weight_col[0:64], pairs[0:64, :, :, 0])
                    link(nc.vector.tensor_copy(weight_col[64:P], pairs[64:P, :, :, 1]))

            def residual(i):
                dve.wait_ge(x_res_set, i)
                for f in (WO0, WO1):
                    k = f - WO0
                    dve.wait_ge(tail_mm[k], fills(i, f) + 1)
                    nc.vector.tensor_tensor(x_mid[:, 2 * k:2 * k + 2],
                                            tails[k][:].rearrange("p (b d) -> p b d", b=2),
                                            x_res[:, 2 * k:2 * k + 2], ALU.add).then_inc(tail_free[k], 1)

            def cross_residual(i, f):
                dve.wait_ge(tail_mm[f % 2], fills(i, f) + 1)
                for m in range(2):
                    b = 2 * (f - AV0) + m
                    ins = nc.vector.scalar_tensor_tensor(
                        out=x_mid[:, b], in0=tails[f % 2][:, D * m:D * m + D], scalar=prob_rsum[:, b:b + 1],
                        in1=x_mid[:, b], op0=ALU.mult, op1=ALU.add)
                ins.then_inc(tail_free[f % 2], 1)

            def last_residual(i, f):
                dve.wait_ge(out_free, 16 * i)
                k = f - UP0
                dve.wait_ge(tail_mm[k], fills(i, f) + 1)
                nc.vector.tensor_tensor(out_sb[:, 2 * k:2 * k + 2],
                                        tails[k][:].rearrange("p (b d) -> p b d", b=2),
                                        x_mid[:, 2 * k:2 * k + 2], ALU.add).then_inc(tail_free[k], 1)

            def weigh(i, j):
                dve.wait_ge(tail_free[(H0 + j) % 2], fills(i, H0 + j) + 1)
                hj = hidden[:, j].rearrange("p (b t) -> p b t", b=GB)
                nc.vector.tensor_tensor(hj, hj, weight_col[:, j].unsqueeze(2).broadcast_to([P, GB, T]),
                                        ALU.mult).then_inc(weighted, 1)

            def tail_part(i, s, slot):
                at = (s, slot)
                if at == (0, 2):
                    for f in (WO0, WO1):
                        dve.wait_ge(tail_free[f % 2], fills(i, f) + 1)
                    ln_stats(i, 1, x_mid)
                if at == (0, 3):
                    ln_variance(i, 1)
                if at == (0, 5):
                    ln_normalize(i, 1, x_mid)
                if at == (1, 5):
                    dve.wait_ge(tail_mm[0], fills(i, SCORES) + 1)
                    nc.vector.tensor_reduce(row_max[:], tail0[:].rearrange("p (b t) -> p b t", b=GB), AX,
                                            ALU.max).then_inc(row_stat, 1)
                    dve.wait_ge(row_stat, 2 * (i - 1) + 1)
                    nc.vector.tensor_scalar(neg_max[:], row_max[:], -1.0, None, ALU.mult).then_inc(max_set, 1)
                if at == (2, 2):
                    dve.wait_ge(tail_free[0], fills(i, SCORES) + 1)
                    nc.vector.reciprocal(prob_rsum[:], prob_sum[:]).then_inc(row_stat, 1)
                if at == (2, 5):
                    dve.wait_ge(row_stat, 2 * (i - 1) + 2)
                    cross_residual(i, AV0)
                if at == (2, 6):
                    cross_residual(i, AV1)
                if at == (3, 1):
                    for f in (AV0, AV1):
                        dve.wait_ge(tail_free[f % 2], fills(i, f) + 1)
                    ln_stats(i, 2, x_mid)
                if at == (3, 2):
                    ln_variance(i, 2)
                if at == (3, 4):
                    ln_normalize(i, 2, x_mid)
                if s == 4 and slot in (2, 3):
                    c = slot - 2
                    dve.wait_ge(tail_free[c], fills(i, X3T0 + c) + 1)
                    nc.vector.tensor_reduce(pooled[:, GB * c:GB * c + GB],
                                            xnT2[:, c].rearrange("p (b t) -> p b t", b=GB), AX,
                                            ALU.add).then_inc(pooled_set, 1)
                if at == (5, 1):
                    dve.wait_ge(tail_mm[0], fills(i, GATE) + 1)
                    nc.vector.tensor_scalar(logits[:].rearrange("p b e -> p (b e)"), tail0[:, 0:GB * E], 1.0 / T, None,
                                            ALU.mult).then_inc(tail_free[0], 1)
                    dve.wait_ge(tail_free[0], fills(i, GATE) + 1)
                    nc.vector.tensor_reduce(gate_max[:], logits[:], AX, ALU.max).then_inc(gate_max_set, 1)
                    dve.wait_ge(gate_max_set, i)
                    nc.vector.tensor_tensor(logits[:], logits[:], gate_max[:].unsqueeze(2).broadcast_to([P, GB, E]),
                                            ALU.subtract).then_inc(logits_set, 1)
                if s == 5 and slot in (4, 5, 6):
                    softmaxed_gate(i, slot - 4)
                if s == 6 and slot in (1, 2, 3, 4):
                    weigh(i, slot - 1)
                if at == (7, 0):
                    dve.wait_ge(tail_mm[1], fills(i, WT) + 1)
                    nc.vector.tensor_copy(weightT[:].rearrange("e b t -> e (b t)"), tail1[0:E, :]).then_inc(tail_free[1], 1)
                if at == (7, 3):
                    last_residual(i, UP0)
                if at == (7, 5):
                    last_residual(i, UP1)

            def split_weights(k):
                dve.wait_ge(w_hi, k + 1)
                parts, whole = staged[k]
                upper = parts[:, HI].bitcast(F32).rearrange("p c n -> p (c n)")
                nc.vector.tensor_tensor(parts[:, LO].rearrange("p c n -> p (c n)"), whole, upper,
                                        ALU.subtract).then_inc(w_split, 1)

            def body(i, tail, first=False):
                dve.wait_ge(x_in, 16 * (i + 1))
                ln_stats(i, 0, x_next)
                ln_variance(i, 0)
                ln_normalize(i, 0, x_next)
                for c in range(KC):
                    dve.wait_ge(xT_hi, KC * i + c + 1)
                    nc.vector.tensor_tensor(xnT[:, LO, c], tails[c][:], xnT[:, HI, c].bitcast(F32),
                                            ALU.subtract).then_inc(tail_free[c], 1)
                if first:
                    for k in range(4):
                        split_weights(k)
                if tail:
                    o_scaled(i * H - 1, (H - 1) % 2)
                squares_in(i * H)
                if tail:
                    residual(i)
                for h in range(H):
                    n, par, more = i * H + h, h % 2, h < H - 1
                    if tail:
                        tail_part(i, h, 0)
                    for l in range(1, LEVELS):
                        decay(n, par, l)
                        if l == 3:
                            mask(n, 0)
                        if l == 4 and h > 0:
                            o_scaled(n - 1, 1 - par)
                        if l == 5 and more:
                            squares_in(n + 1)
                        if l == 6:
                            mask(n, 1)
                        if tail:
                            tail_part(i, h, l)

            dve.wait_ge(c_in, N_C)
            body(0, False, first=True)
            with dve.Fori(1, NG) as i:
                body(i, True)
            o_scaled(NG * H - 1, (H - 1) % 2)
            residual(NG)
            for s in range(H):
                for slot in range(LEVELS):
                    tail_part(NG, s, slot)

        @block.tensor
        def _(pe):
            mm = nc.tensor.matmul
            PARTS = ((HI, HI), (HI, LO), (LO, HI))

            def project(w, dst, h):
                for c in range(KC):
                    for k, (a, b) in enumerate(PARTS):
                        last = mm(dst[:], w[:, a, c, P * h:P * h + P], xnT[:, b, c], start=(c == 0 and k == 0),
                                  stop=(c == KC - 1 and k == 2))
                return last

            def project_g(i, h):
                n = i * H + h
                positive(pe, v_raw_set, n + (1 if h > 0 else 0))
                project(wg_sb, bank_gv, h).then_inc(g_mm, 1)

            def project_q(n, h):
                positive(pe, attnT_set, n - (1 if h > 0 else 0))
                project(wq_sb, bank_q, h).then_inc(q_mm, 1)

            def project_k(n, h):
                positive(pe, norm_sq_set, n)
                project(wk_sb, bank_k, h).then_inc(k_mm, 1)

            def project_v(i, m):
                pair, half = m // 2, m % 2
                if m != 1:
                    pe.wait_ge(alpha_set, i * H + max(m, 1))
                else:
                    pe.wait_ge(v_raw_set, i * H + 1)
                for k in range(2):
                    b = 2 * half + k
                    for c in range(KC):
                        for part, (a, w) in enumerate(PARTS):
                            last = mm(bank_gv[:, 2 * P * k:2 * P * k + 2 * P], xnT[:, a, c, T * b:T * b + T],
                                      wv_sb[:, w, c, 2 * P * pair:2 * P * pair + 2 * P],
                                      start=(c == 0 and part == 0), stop=(c == KC - 1 and part == 2))
                last.then_inc(v_mm, 1)

            def norms(n, par):
                pe.wait_ge(q_set, n + 1)
                pe.wait_ge(k_set, n + 1)
                block_products(bank_k, 0, q_raw[:, par], q_raw[:, par])
                block_products(bank_k, 1, qk_dec[:, par, 1], qk_dec[:, par, 1]).then_inc(norm_mm, 1)

            def block_products(dst, slot, left, right):
                for b in range(GB):
                    for r in range(T // BLOCK):
                        at = T * b + BLOCK * r
                        to = slot * GB * BLOCK + b * BLOCK
                        last = mm(dst[BLOCK * r:BLOCK * r + BLOCK, to:to + BLOCK], left[:, at:at + BLOCK],
                                  right[:, at:at + BLOCK], start=True, stop=True)
                return last

            def level(n, par, l, more):
                q, k = qk_dec[:, par, 0], qk_dec[:, par, 1]
                if l > 0:
                    pe.wait_ge(decayed, OUTER * n + l)
                if l == 0:
                    pe.wait_ge(level0_set, n + 1)
                    pe.wait_ge(k_set, n + 1)
                    pe.wait_ge(q_set, n + 1)
                    positive(pe, masked, 2 * n)
                    block_products(bank_lo, 0, k, q_raw[:, par])
                    last = block_products(bank_lo, 1, k, q)
                elif l < 3:
                    last = block_products(bank_lo, l + 1, k, q)
                elif l < INNER:
                    last = block_products(bank_hi, l - 3, k, q)
                else:
                    if l == INNER:
                        pe.wait_ge(q_set, n + (2 if more else 1))
                    w = 2 ** l
                    for b in range(GB):
                        for s in range(0, T, 2 * w):
                            at, to = T * b + s, (0 if l == INNER else GB * BLOCK) + w * b
                            last = mm(bank_q[s:s + w, to:to + w], k[:, at:at + w], q[:, at + w:at + 2 * w],
                                      start=True, stop=True)
                last.then_inc(level_mm, 1)

            def attend(n, par):
                positive(pe, oT_set, n)
                pe.wait_ge(attnT_set, n + 1)
                pe.wait_ge(v_set, n + 1)
                for b in range(GB):
                    last = mm(bank_o[:, P * b:P * b + P], attnT[:, b], v_sb[:, par, b], start=True, stop=True)
                last.then_inc(o_mm, 1)

            def attend_transposed(n):
                pe.wait_ge(o_set, n + 1)
                for b in range(GB):
                    last = nc.tensor.transpose(bank_o[:, P * b:P * b + P], o_sb[:, b], ident[:])
                last.then_inc(oT_mm, 1)

            def fill(i, f):
                positive(pe, tail_free[f % 2], fills(i, f))
                return tails[f % 2]

            def transposed(i, f0):
                for c in range(KC):
                    dst = fill(i, f0 + c)
                    for b in range(GB):
                        last = nc.tensor.transpose(dst[:, T * b:T * b + T], xn[:, b, P * c:P * c + P], ident[:])
                    last.then_inc(tail_mm[(f0 + c) % 2], 1)

            def cross_keys(i):
                pe.wait_ge(ctxT_in, 16 * KC * (i + 1))
                for f in (KEY0, KEY1):
                    j = f - KEY0
                    dst = fill(i, f)
                    for c in range(KC):
                        last = mm(dst[:], xw_sb[:, c, P * j:P * j + P], ctxT_sb[:, c].rearrange("p b t -> p (b t)"),
                                  start=(c == 0), stop=(c == KC - 1))
                    last.then_inc(tail_mm[j], 1)

            def output_projection(i):
                pe.wait_ge(oT_set, H * i)
                for f in (WO0, WO1):
                    dst = fill(i, f)
                    for m in range(2):
                        b = 2 * (f - WO0) + m
                        for h in range(H):
                            last = mm(dst[:, D * m:D * m + D], oT_sb[:, h, T * b:T * b + T], wo_sb[:, h],
                                      start=(h == 0), stop=(h == H - 1))
                    last.then_inc(tail_mm[f % 2], 1)

            def up_projection(i, b):
                k, m = b // 2, b % 2
                dst = tails[k]
                if m == 0:
                    pe.wait_ge(weighted, EJ * i)
                    pe.wait_ge(tail_free[1], fills(i, WT) + 1)
                    fill(i, UP0 + k)
                for j in range(EJ):
                    mm(dst[:, D * m:D * m + D], hidden[:, j, T * b:T * b + T], up_sb[:, j],
                       start=(j == 0), stop=False)
                last = mm(dst[:, D * m:D * m + D], weightT[:, b], upb_sb[:], start=False, stop=True)
                if m == 1:
                    last.then_inc(tail_mm[k], 1)

            def tail_middle(i, s):
                if s == 1:
                    pe.wait_ge(tail_free[0], fills(i, X2T0) + 1)
                    pe.wait_ge(tail_free[1], fills(i, X2T1) + 1)
                    dst = fill(i, SCORES)
                    for b in range(GB):
                        for c in range(KC):
                            last = mm(dst[:, T * b:T * b + T], xnT2[:, c, T * b:T * b + T], projT[:, c, b],
                                      start=(c == 0), stop=(c == KC - 1))
                    last.then_inc(tail_mm[0], 1)
                if s == 2:
                    pe.wait_ge(tail_free[1], fills(i, PT) + 1)
                    pe.wait_ge(ctx_in, 16 * i)
                    for f in (AV0, AV1):
                        dst = fill(i, f)
                        for m in range(2):
                            b = 2 * (f - AV0) + m
                            last = mm(dst[:, D * m:D * m + D], probsT[:, b], ctx_sb[:, b], start=True, stop=True)
                        last.then_inc(tail_mm[f % 2], 1)

            def tail_last(i, s):
                if s == 0 or s == 3:
                    pe.wait_ge(ln_out, norms_done(i, 1 if s == 0 else 2) + 1)
                    transposed(i, X2T0 if s == 0 else X3T0)
                if s == 1:
                    pe.wait_ge(tail_free[0], fills(i, SCORES) + 1)
                    dst = fill(i, PT)
                    for b in range(GB):
                        last = nc.tensor.transpose(dst[:, T * b:T * b + T], probs[:, b], ident[:])
                    last.then_inc(tail_mm[1], 1)
                if s == 4:
                    pe.wait_ge(pooled_set, KC * i)
                    dst = fill(i, GATE)
                    for b in range(GB):
                        for c in range(KC):
                            last = mm(dst[:, E * b:E * b + E],
                                      pooled[:, GB * c + b:GB * c + b + 1].broadcast_to([P, P]), gate_sb[:, c],
                                      start=(c == 0), stop=(c == KC - 1))
                    last.then_inc(tail_mm[0], 1)
                if s == 4 or s == 5:
                    for f in (H0,) if s == 4 else (H1, H2, H3):
                        j = f - H0
                        dst = fill(i, f)
                        for c in range(KC):
                            last = mm(dst[:], down_sb[:, c, P * j:P * j + P], xnT2[:, c], start=(c == 0),
                                      stop=(c == KC - 1))
                        last.then_inc(tail_mm[f % 2], 1)
                if s == 6:
                    pe.wait_ge(small, 11 * i)
                    dst = fill(i, WT)
                    for b in range(GB):
                        last = nc.tensor.transpose(dst[0:E, T * b:T * b + T], weight[:, b], ident[:])
                    last.then_inc(tail_mm[1], 1)

            def body(i, tail, first=False):
                n = i * H
                pe.wait_ge(ln_out, norms_done(i, 0) + 1)
                transposed(i, XT0)
                if tail:
                    attend(n - 1, (H - 1) % 2)
                pe.wait_ge(tail_free[1], fills(i, XT1) + 1)
                pe.wait_ge(tail_free[0], fills(i, XT0) + 1)
                if first:
                    pe.wait_ge(w_split, 1)
                project_g(i, 0)
                if first:
                    pe.wait_ge(w_split, 2)
                project_q(n, 0)
                if first:
                    pe.wait_ge(w_split, 3)
                project_k(n, 0)
                if tail:
                    attend_transposed(n - 1)
                if first:
                    pe.wait_ge(w_split, 4)
                project_v(i, 0)
                norms(n, 0)
                project_v(i, 1)
                if tail:
                    output_projection(i)
                for h in range(H):
                    n, par, more = i * H + h, h % 2, h < H - 1
                    up = tail and not more
                    level(n, par, 0, more)
                    if more:
                        project_g(i, h + 1)
                    if up:
                        up_projection(i, 0)
                    level(n, par, 1, more)
                    if more:
                        project_q(n + 1, h + 1)
                    if up:
                        up_projection(i, 1)
                    level(n, par, 2, more)
                    if more:
                        project_k(n + 1, h + 1)
                    if up:
                        up_projection(i, 2)
                    level(n, par, 3, more)
                    if h > 0:
                        attend(n - 1, 1 - par)
                    if tail:
                        tail_middle(i, h)
                    level(n, par, 4, more)
                    if more:
                        norms(n + 1, 1 - par)
                    if up:
                        up_projection(i, 3)
                    level(n, par, 5, more)
                    if h + 2 < H:
                        project_v(i, h + 2)
                    level(n, par, 6, more)
                    if h > 0:
                        attend_transposed(n - 1)
                    if tail:
                        tail_last(i, h)
                if first:
                    pe.wait_ge(w_in, N_W)
                cross_keys(i)

            pe.wait_ge(c_in, N_C)
            pe.wait_ge(consts_set, 1)
            body(0, False, first=True)
            with pe.Fori(1, NG) as i:
                body(i, True)
            attend(NG * H - 1, (H - 1) % 2)
            attend_transposed(NG * H - 1)
            output_projection(NG)
            for s in range(H):
                tail_middle(NG, s)
                tail_last(NG, s)
            for b in range(GB):
                up_projection(NG, b)


def kernel(x, ctx_1024, L0_attn_Wq, L0_attn_Wk, L0_attn_Wv, L0_attn_Wg, L0_attn_Wo, L0_xattn_W,
           L0_ffn_gate_w, L0_ffn_down_w, L0_ffn_down_b, L0_ffn_up_w, L0_ffn_up_b):
    import concourse.bacc as bacc
    from concourse.bass_utils import run_bass_kernel_spmd

    E, BN, D = L0_ffn_down_w.shape
    ident, owned, experts = shape_constants(4)
    arrays = {
        "x": x,
        "ctx": ctx_1024,
        "ctxT": np.transpose(ctx_1024, (0, 2, 1)),
        "wq": L0_attn_Wq, "wk": L0_attn_Wk, "wv": L0_attn_Wv, "wg": L0_attn_Wg, "wo": L0_attn_Wo,
        "xwT": np.transpose(L0_xattn_W),
        "gateT": np.transpose(L0_ffn_gate_w),
        "downT": np.transpose(np.reshape(L0_ffn_down_w, (E * BN, D))),
        "down_b": np.transpose(np.reshape(L0_ffn_down_b, (E * BN // P, P))),
        "up": np.reshape(np.transpose(L0_ffn_up_w, (0, 2, 1)), (E * BN, D)),
        "up_b": L0_ffn_up_b,
        "ident_c": ident, "owned_c": owned, "experts_c": experts,
    }
    arrays = {name + "_dram": np.ascontiguousarray(a) for name, a in arrays.items()}
    nc = bacc.Bacc("TRN2", target_bir_lowering=False, num_devices=1)
    args = [nc.dram_tensor(name, a.shape, mybir.dt.from_np(a.dtype), kind="ExternalInput").ap()
            for name, a in arrays.items()]
    out = nc.dram_tensor("out_dram", x.shape, F32, kind="ExternalOutput").ap()
    decoder_kernel(nc, *args, out)
    r = run_bass_kernel_spmd(nc, [arrays], core_ids=[0])
    return r.results[0]["out_dram"]
```

```python
from contextlib import ExitStack

import numpy as np

import concourse.bass as bass
from concourse import mybir

P = 128
F32 = mybir.dt.float32
F32R = mybir.dt.float32r
U32 = mybir.dt.uint32
ALU = mybir.AluOpType
ACT = mybir.ActivationFunctionType
AX = mybir.AxisListType.X

LN_EPS = 1e-5
NORM_EPS = 1e-12
TOPW_EPS = 1e-8
LEVELS = 7
BLOCK = 32
OUTER = LEVELS - 1
INNER = 5


def shape_constants(sequences):
    ident = np.eye(P, dtype=np.float32)
    s = np.arange(P)[:, None] % BLOCK
    t = np.arange(BLOCK)[None, :]
    owned = [s == t] + [((s >> (l + 1)) == (t >> (l + 1))) & ((s >> l) % 2 == 0) & ((t >> l) % 2 == 1)
                        for l in range(INNER)]
    owned = np.stack([np.tile(m, (1, sequences)) for m in owned], axis=1).astype(np.float32)
    experts = np.broadcast_to(np.arange(8, dtype=np.float32), (P, 8)).copy()
    return ident, owned, experts


def decoder_kernel(nc, x, ctx, ctxT, wq, wk, wv, wg, wo, xwT, gateT, downT, down_b, up, up_b,
                   ident_c, owned_c, experts_c, out):
    B, T, D = x.shape
    H = wq.shape[1] // P
    KC = D // P
    GB = 4
    NG = B // GB
    N = GB * T
    E = gateT.shape[1]
    EJ = downT.shape[1] // P
    assert T == P and D == 256 and N == 512 and E == 8

    with ExitStack() as stack:
        def sb(name, shape, dt=F32):
            return stack.enter_context(nc.sbuf_tensor(name, shape, dt))

        def bank(name):
            return stack.enter_context(nc.psum_tensor(name, [P, 512], F32))

        def sem(name):
            return stack.enter_context(nc.semaphore(name))

        HI, LO = 0, 1
        wq_sb, wk_sb, wv_sb, wg_sb = (
            sb(n, [P, 2, KC, H * P], F32R) for n in ("wq_sb", "wk_sb", "wv_sb", "wg_sb"))
        wo_sb = sb("wo_sb", [P, H, D])
        xw_sb = sb("xw_sb", [P, KC, D])
        gate_sb = sb("gate_sb", [P, KC, E])
        down_sb = sb("down_sb", [P, 2, KC, EJ * P], F32R)
        downb_sb = sb("downb_sb", [P, EJ])
        up_sb = sb("up_sb", [P, EJ, D])
        upb_sb = sb("upb_sb", [E, D])
        ident = sb("ident", [P, P])
        N_IN = GB * BLOCK
        owned = sb("owned", [P, 1 + INNER, N_IN])
        experts = sb("experts", [P, E])
        ones = sb("ones", [P, 1])
        scratch = sb("scratch", [P, 1])
        pool_scratch = sb("pool_scratch", [P, 1])
        neg_half = sb("neg_half", [P, 8])
        x_next = sb("x_next", [P, GB, D])
        x_res = sb("x_res", [P, GB, D])
        ctx_sb = sb("ctx_sb", [P, GB, D])
        ctxT_sb = sb("ctxT_sb", [P, KC, GB, T])
        stats = sb("stats", [P, GB, 6])
        mean_var = sb("mean_var", [P, GB, 2])
        var_eps = sb("var_eps", [P, GB])
        rstd = sb("rstd", [P, GB])
        xn = sb("xn", [P, GB, D])
        xnT = sb("xnT", [P, 2, KC, N], F32R)
        alpha = sb("alpha", [P, 2, N])
        q_raw = sb("q_raw", [P, 2, N])
        qk_dec = sb("qk_dec", [P, 2, 2, N])
        self_diag = sb("self_diag", [P, 2 * GB, BLOCK])
        spans = sb("spans", [P, N])
        self_sq = sb("self_sq", [P, 2 * GB])
        norm_sq = sb("norm_sq", [P, 2, GB])
        rnorm = sb("rnorm", [P, 2, 2, GB])
        v_raw = sb("v_raw", [P, 2, GB, 2, P])
        v_sb = sb("v_sb", [P, 2, GB, P])
        by_level = sb("by_level", [P, 1 + INNER, GB, BLOCK])
        blocks = sb("blocks", [P, GB, BLOCK])
        attnT = sb("attnT", [P, GB, T])
        o_sb = sb("o_sb", [P, GB, P])
        oT_sb = sb("oT_sb", [P, H, N])
        x_mid = sb("x_mid", [P, GB, D])
        projT = sb("projT", [P, KC, GB, T])
        row_max = sb("row_max", [P, GB])
        neg_max = sb("neg_max", [P, GB])
        prob_sum = sb("prob_sum", [P, GB])
        prob_rsum = sb("prob_rsum", [P, GB])
        pooled = sb("pooled", [P, KC, GB])
        gated = sb("gated", [P, KC, GB, E])
        logits = sb("logits", [P, GB, E])
        gate_max = sb("gate_max", [P, GB])
        gate_exp = sb("gate_exp", [P, GB, E])
        gate_sum = sb("gate_sum", [P, GB])
        top_val = sb("top_val", [P, GB, 8])
        top_idx = sb("top_idx", [P, GB, 8], U32)
        top_num = sb("top_num", [P, GB, 8])
        is_first = sb("is_first", [P, GB, E])
        is_second = sb("is_second", [P, GB, E])
        top_sum = sb("top_sum", [P, GB])
        weight = sb("weight", [P, GB, E])
        weight_col = sb("weight_col", [P, EJ, GB])
        weightT = sb("weightT", [E, GB, T])
        x3T = sb("x3T", [P, 2, KC, N], F32R)
        hidden = sb("hidden", [P, EJ, N])
        x2T = hidden[:, 0:KC]
        probs, probsT = (hidden[:, KC + k].rearrange("p (b t) -> p b t", b=GB) for k in range(2))
        out_sb = sb("out_sb", [P, GB, D])

        stage_g = hidden[:, 0:EJ].rearrange("p j n -> p (j n)")
        stage_q = oT_sb[:, 0:4].rearrange("p h n -> p (h n)")
        stage_k = oT_sb[:, 4:8].rearrange("p h n -> p (h n)")
        stage_v = v_raw[:].rearrange("p r b h v -> p (r b h v)")
        stage_down = x_mid[:].rearrange("p b d -> p (b d)")
        staged = ((wg_sb, stage_g), (wq_sb, stage_q), (wk_sb, stage_k), (wv_sb, stage_v), (down_sb, stage_down))
        DOWN = 4

        bank_q, bank_k, bank_gv, bank_lo, bank_hi, bank_o, tail0, tail1 = (
            bank(n) for n in ("bank_q", "bank_k", "bank_gv", "bank_lo", "bank_hi", "bank_o", "tail0", "tail1"))
        tails = (tail0, tail1)

        w_hi, w_split, xT_hi = sem("w_hi"), sem("w_split"), sem("xT_hi")
        wg_in, wq_in, wk_in, wv_in, down_in = (sem(n) for n in ("wg_in", "wq_in", "wk_in", "wv_in", "down_in"))
        x3T_hi = sem("x3T_hi")
        w_in, c_in, x_in, ctx_in, ctxT_in, out_free = (
            sem(n) for n in ("w_in", "c_in", "x_in", "ctx_in", "ctxT_in", "out_free"))
        ident_in, consts_set = sem("ident_in"), sem("consts_set")
        g_mm, q_mm, k_mm, v_mm, norm_mm, level_mm, o_mm, oT_mm = (
            sem(n) for n in ("g_mm", "q_mm", "k_mm", "v_mm", "norm_mm", "level_mm", "o_mm", "oT_mm"))
        tail_mm = (sem("tail_mm0"), sem("tail_mm1"))
        tail_free = (sem("tail_free0"), sem("tail_free1"))
        alpha_set, q_set, k_set, oT_set, attnT_set = (
            sem(n) for n in ("alpha_set", "q_set", "k_set", "oT_set", "attnT_set"))
        gate_exp_set = sem("gate_exp_set")
        self_set, v_raw_set = sem("self_set"), sem("v_raw_set")
        level0_set, decayed, span_set, masked, blocks_set, norm_sq_set, v_set, o_set = (
            sem(n) for n in ("level0_set", "decayed", "span_set", "masked", "blocks_set", "norm_sq_set",
                             "v_set", "o_set"))
        ln_stat, ln_var, ln_out = sem("ln_stat"), sem("ln_var"), sem("ln_out")
        ln_rstd, rnorm_set, x_res_set = sem("ln_rstd"), sem("rnorm_set"), sem("x_res_set")
        half_mm, half_out, half_row, half_rstd = (
            (sem(n + "0"), sem(n + "1")) for n in ("half_mm", "half_out", "half_row", "half_rstd"))
        row_stat, max_set, pooled_set, gated_set, gate_max_set, logits_set, small, weighted = (
            sem(n) for n in ("row_stat", "max_set", "pooled_set", "gated_set", "gate_max_set", "logits_set",
                             "small", "weighted"))

        (XT0, XT1, WO0, WO1, X2T0, X2T1, SCORES, PT, AV0, AV1, X3T0, X3T1,
         GATE, H0, H1, H2, H3, WT, KEY0, UPA, UPB, KEY1) = range(22)

        def fills(i, f):
            if isinstance(i, int) and i == 0:
                return 0 if f <= XT1 else 1
            left_out = 0
            if isinstance(i, int) and i == NG:
                left_out = 7 if f == UPB else 6
            return 11 * i - 9 + f // 2 - left_out

        def norms_done(i, k):
            if isinstance(i, int) and i == 0:
                return 0
            return 3 * i - 2 + k

        (MM_WO, MM_X2T, MM_SCORES, MM_PT, MM_AV, MM_X3T) = range(1, 7)
        (TO_X2T, TO_PROBS, TO_PT, TO_X3T) = range(1, 5)
        (AT_MID, AT_STATS, AT_MEAN, AT_VAR, AT_XN, AT_MAX, AT_NEG_MAX, AT_RSUM,
         AT_MID2, AT_STATS2, AT_MEAN2, AT_VAR2, AT_XN2, AT_POOLED, AT_X3T) = range(1, 16)
        half_bank = ((bank_k, bank_q), (bank_lo, bank_hi))

        def positive(engine, s, value):
            if not isinstance(value, int) or value > 0:
                engine.wait_ge(s, value)

        def view(tensor, start, dims):
            whole = tensor[:]
            return bass.AP(whole.tensor, whole.offset + start, [list(whole.ap[0])] + dims)

        SMALL = 11
        N_W, N_C = 16 * 6, 16 * 2

        block = stack.enter_context(nc.Block())

        @block.sync
        def _(sp):
            def load_x(i):
                sp.dma_start(x_next[:], x[bass.ts(i, GB)].rearrange("b t d -> t b d")).then_inc(x_in, 16)

            def load_ctxT(i):
                for c in range(KC):
                    sp.dma_start(ctxT_sb[:, c], ctxT[bass.ts(i, GB), P * c:P * c + P].rearrange("b p t -> p b t")
                                 ).then_inc(ctxT_in, 16)

            def load_ctx(i):
                sp.dma_start(ctx_sb[:], ctx[bass.ts(i, GB)].rearrange("b t d -> t b d")).then_inc(ctx_in, 16)

            load_x(0)
            sp.dma_start(ident[:], ident_c).then_inc(ident_in, 16)
            for dst, src, s in ((stage_g, wg, wg_in), (stage_q, wq, wq_in), (stage_k, wk, wk_in),
                                (stage_v, wv, wv_in)):
                sp.dma_start(dst.rearrange("p (c n) -> p c n", c=KC),
                             src.rearrange("(c p) n -> p c n", p=P)).then_inc(s, 16)
            for dst, src in ((owned, owned_c), (experts, experts_c)):
                sp.dma_start(dst[:], src).then_inc(c_in, 16)
            load_ctxT(0)
            load_ctx(0)
            sp.dma_start(wo_sb[:], wo.rearrange("(h p) n -> p h n", p=P)).then_inc(w_in, 16)
            for dst, src in ((xw_sb, xwT), (gate_sb, gateT)):
                sp.dma_start(dst[:], src.rearrange("(c p) n -> p c n", p=P)).then_inc(w_in, 16)
            sp.dma_start(stage_down.rearrange("p (c n) -> p c n", c=KC),
                         downT.rearrange("(c p) n -> p c n", p=P)).then_inc(down_in, 16)
            sp.dma_start(downb_sb[:], down_b).then_inc(w_in, 16)
            sp.dma_start(up_sb[:], up.rearrange("(j p) n -> p j n", p=P)).then_inc(w_in, 16)
            sp.dma_start(upb_sb[:], up_b).then_inc(w_in, 16)
            sp.wait_ge(ln_out, 1)
            sp.wait_ge(x_res_set, 1)
            load_x(1)

            def store(i):
                ended = isinstance(i, int) and i == NG
                for f in (UPB, UPA if ended else KEY1):
                    sp.wait_ge(tail_free[f % 2], fills(i, f) + 1)
                sp.dma_start(out[bass.ts(i - 1, GB)].rearrange("b t d -> t b d"), out_sb[:]).then_inc(out_free, 16)

            def body(i, last):
                sp.wait_ge(tail_mm[1], fills(i, XT1))
                load_ctxT(i)
                if not last:
                    sp.wait_ge(x_res_set, i + 1)
                    sp.wait_ge(ln_out, norms_done(i, 0) + 1)
                    load_x(i + 1)
                sp.wait_ge(tail_mm[1], fills(i, AV1) + 1)
                load_ctx(i)
                store(i)

            with sp.Fori(1, NG - 1) as i:
                body(i, False)
            body(NG - 1, True)
            store(NG)
            sp.wait_ge(out_free, 16 * (NG + 1))

        @block.gpsimd
        def _(pool):
            nc.gpsimd.memset(neg_half[:], -0.5)
            nc.gpsimd.memset(ones[:], 1.0)
            nc.gpsimd.memset(out_sb[:], 0.0).then_inc(out_free, 16)
            nc.gpsimd.memset(attnT[:], 0.0).then_inc(consts_set, 1)
            pool.wait_ge(consts_set, 1)

            def ln_power(i, k):
                pool.wait_ge(ln_var, norms_done(i, k) + 1)
                positive(pool, ln_out, norms_done(i, k))
                nc.gpsimd.tensor_tensor(rstd[:], var_eps[:], neg_half[:, 0:GB], ALU.pow).then_inc(ln_rstd, 1)

            def keep_x(i):
                pool.wait_ge(x_in, 16 * (i + 1))
                if not (isinstance(i, int) and i == 0):
                    for f in (WO0, WO1):
                        pool.wait_ge(tail_free[f % 2], fills(i, f) + 1)
                nc.gpsimd.tensor_tensor(pool_scratch[:], neg_half[:, 0:1], neg_half[:, 0:1], ALU.mult)
                nc.gpsimd.tensor_copy(x_res[:], x_next[:]).then_inc(x_res_set, 1)

            def reciprocal_norms(n, par):
                pool.wait_ge(norm_sq_set, n + 1)
                if not (isinstance(n, int) and n < 2):
                    pool.wait_ge(v_set, n - 1)
                    pool.wait_ge(o_set, n - 1)
                nc.gpsimd.tensor_tensor(rnorm[:, par].rearrange("p a b -> p (a b)"),
                                        norm_sq[:].rearrange("p a b -> p (a b)"), neg_half[:],
                                        ALU.pow).then_inc(rnorm_set, 1)

            def q_decayed(n, par):
                pool.wait_ge(q_set, n + 1)
                pool.wait_ge(alpha_set, n + 1)
                if not (isinstance(n, int) and n < 2):
                    pool.wait_ge(level_mm, LEVELS * (n - 1))
                nc.gpsimd.tensor_tensor(qk_dec[:, par, 0], q_raw[:, par], alpha[:, par], ALU.mult).then_inc(level0_set, 1)

            def v_scaled(i, h):
                n, par = i * H + h, h % 2
                pool.wait_ge(v_raw_set, i * H + h // 2 * 2 + 2)
                pool.wait_ge(rnorm_set, n + 1)
                if not (isinstance(n, int) and n < 2):
                    pool.wait_ge(o_mm, n - 1)
                nc.gpsimd.tensor_tensor(v_sb[:, par], v_raw[:, h // 2 % 2, :, par],
                                        rnorm[:, par, 1].unsqueeze(2).broadcast_to([P, GB, P]),
                                        ALU.mult).then_inc(v_set, 1)

            def weigh(i, j):
                pool.wait_ge(tail_free[(H0 + j) % 2], fills(i, H0 + j) + 1)
                pool.wait_ge(small, SMALL * i)
                hj = hidden[:, j].rearrange("p (b t) -> p b t", b=GB)
                nc.gpsimd.tensor_tensor(hj, hj, weight_col[:, j].unsqueeze(2).broadcast_to([P, GB, T]),
                                        ALU.mult).then_inc(weighted, 1)

            def body(i, tail, last=False):
                q_decayed(i * H, 0)
                reciprocal_norms(i * H, 0)
                v_scaled(i, 0)
                keep_x(i)
                for h in range(H):
                    if h < H - 1:
                        q_decayed(i * H + h + 1, (h + 1) % 2)
                    if tail and h == 0:
                        ln_power(i, 1)
                    if tail and h == 3:
                        ln_power(i, 2)
                    if tail and h == 6:
                        for j in range(EJ):
                            weigh(i, j)
                    if h < H - 1:
                        reciprocal_norms(i * H + h + 1, (h + 1) % 2)
                        v_scaled(i, h + 1)
                if not last:
                    ln_power(i + 1, 0)

            ln_power(0, 0)
            body(0, False)
            with pool.Fori(1, NG - 1) as i:
                body(i, True)
            body(NG - 1, True, last=True)
            for z, step in ((0, 1), (1, 1), (0, 2), (1, 2)):
                pool.wait_ge(half_row[z], AT_VAR if step == 1 else AT_VAR2)
                nc.gpsimd.tensor_tensor(rstd[:, 2 * z:2 * z + 2], var_eps[:, 2 * z:2 * z + 2], neg_half[:, 0:2],
                                        ALU.pow).then_inc(half_rstd[z], 1)
            for j in range(EJ // 2):
                weigh(NG, j)

        @block.scalar
        def _(act):
            def head_in(n, par, hook):
                hook("first")
                act.wait_ge(g_mm, n + 1)
                if not (isinstance(n, int) and n < 2):
                    act.wait_ge(level_mm, LEVELS * (n - 1))
                nc.scalar.activation(alpha[:, par], bank_gv[:], ACT.Sigmoid).then_inc(alpha_set, 1)
                hook("alpha")
                act.wait_ge(q_mm, n + 1)
                nc.scalar.copy(q_raw[:, par], bank_q[:]).then_inc(q_set, 1)
                hook("q")
                act.wait_ge(k_mm, n + 1)
                nc.scalar.copy(qk_dec[:, par, 1], bank_k[:]).then_inc(k_set, 1)
                hook("k")

            def v_out(i, m):
                pair, half = m // 2, m % 2
                act.wait_ge(v_mm, i * H + m + 1)
                positive(act, v_set, i * H + 2 * pair - 2)
                nc.scalar.copy(v_raw[:, pair % 2, 2 * half:2 * half + 2],
                               bank_gv[:].rearrange("p (b h v) -> p b h v", b=2, h=2)).then_inc(v_raw_set, 1)

            def oT_out(n, h):
                act.wait_ge(oT_mm, n + 1)
                nc.scalar.copy(oT_sb[:, h], bank_o[:]).then_inc(oT_set, 1)

            def expand(n):
                positive(act, o_mm, n)
                act.wait_ge(level_mm, LEVELS * (n + 1))
                near = bank_q[:, 0:GB * BLOCK].rearrange("p (b t) -> p b t", b=GB)
                far = bank_q[:, GB * BLOCK:3 * GB * BLOCK].rearrange("p (b t) -> p b t", b=GB)
                for lo in (0, 2 * BLOCK):
                    nc.scalar.copy(attnT[lo:lo + BLOCK, :, lo + BLOCK:lo + 2 * BLOCK], near[lo:lo + BLOCK])
                nc.scalar.copy(attnT[0:T // 2, :, T // 2:T], far[0:T // 2])
                act.wait_ge(blocks_set, n + 1)
                for r in range(T // BLOCK):
                    lo = BLOCK * r
                    last = nc.scalar.copy(attnT[lo:lo + BLOCK, :, lo:lo + BLOCK], blocks[lo:lo + BLOCK])
                last.then_inc(attnT_set, 1)

            def tail_to(dst, i, f):
                act.wait_ge(tail_mm[f % 2], fills(i, f) + 1)
                nc.scalar.copy(dst, tails[f % 2][:]).then_inc(tail_free[f % 2], 1)

            def gelu(i, f):
                j = f - H0
                act.wait_ge(tail_mm[f % 2], fills(i, f) + 1)
                nc.scalar.activation(hidden[:, j], tails[f % 2][:], ACT.Gelu,
                                     bias=downb_sb[:, j:j + 1]).then_inc(tail_free[f % 2], 1)

            def keys_out(i, f):
                tail_to(projT[:, f % 2].rearrange("p b t -> p (b t)"), i, f)

            def tail_part(i, s, place):
                at = (s, place)
                if at == (1, "alpha"):
                    tail_to(x2T[:, 0], i, X2T0)
                    tail_to(x2T[:, 1], i, X2T1)
                if at == (2, "first"):
                    act.wait_ge(max_set, i)
                    for b in range(GB):
                        last = nc.scalar.activation(probs[:, b], tail0[:, T * b:T * b + T], ACT.Exp,
                                                    bias=neg_max[:, b:b + 1], accum_out=prob_sum[:, b:b + 1])
                    last.then_inc(tail_free[0], 1)
                if at == (2, "q"):
                    tail_to(probsT[:].rearrange("p b t -> p (b t)"), i, PT)
                if at == (4, "alpha"):
                    for c in range(KC):
                        act.wait_ge(tail_mm[c], fills(i, X3T0 + c) + 1)
                        nc.scalar.copy(x3T[:, HI, c], tails[c][:]).then_inc(x3T_hi, 1)
                if at == (5, "k"):
                    act.wait_ge(logits_set, i)
                    nc.scalar.activation(gate_exp[:], logits[:], ACT.Exp).then_inc(gate_exp_set, 1)
                    gelu(i, H0)
                if at == (5, "last"):
                    gelu(i, H1)
                    gelu(i, H2)
                if at == (6, "first"):
                    gelu(i, H3)
                if at == (6, "last") and not (isinstance(i, int) and i == NG):
                    keys_out(i, KEY0)

            def split_weights(k):
                act.wait_ge((wg_in, wq_in, wk_in, wv_in, down_in)[k], 16)
                parts, whole = staged[k]
                nc.scalar.copy(parts[:, HI].rearrange("p c n -> p (c n)"), whole).then_inc(w_hi, 1)

            def xnT_upper(i):
                if not (isinstance(i, int) and i == 0):
                    act.wait_ge(v_mm, i * H)
                for c in range(KC):
                    act.wait_ge(tail_mm[c], fills(i, XT0 + c) + 1)
                    nc.scalar.copy(xnT[:, HI, c], tails[c][:]).then_inc(xT_hi, 1)

            def body(i, tail, last=False):
                head_in(i * H, 0, lambda place: None)
                if tail:
                    oT_out(i * H - 1, H - 1)
                v_out(i, 0)
                v_out(i, 1)
                for h in range(H):
                    n = i * H + h
                    def hook(place):
                        if tail:
                            tail_part(i, h, place)

                    if h < H - 1:
                        head_in(n + 1, (h + 1) % 2, hook)
                    if h + 2 < H:
                        v_out(i, h + 2)
                    if not tail and h == H - 2:
                        split_weights(DOWN)
                    if h == H - 1:
                        if not tail:
                            keys_out(i, KEY0)
                        keys_out(i, KEY1)
                        if not last:
                            xnT_upper(i + 1)
                    expand(n)
                    if h > 0:
                        oT_out(n - 1, h - 1)
                    hook("last")

            act.wait_ge(consts_set, 1)
            split_weights(0)
            xnT_upper(0)
            for k in range(1, 4):
                split_weights(k)
            body(0, False)
            act.wait_ge(w_in, N_W)
            with act.Fori(1, NG - 1) as i:
                body(i, True)
            body(NG - 1, True, last=True)
            oT_out(NG * H - 1, H - 1)

            def half_rows(z, step):
                act.wait_ge(half_mm[z], MM_X2T if step == TO_X2T else MM_X3T)
                dst = x2T if step == TO_X2T else x3T[:, HI]
                nc.scalar.copy(dst[:, :, 2 * T * z:2 * T * z + 2 * T],
                               half_bank[z][1][:].rearrange("p (c n) -> p c n", c=KC)).then_inc(half_out[z], 1)

            def half_probs(z):
                act.wait_ge(half_row[z], AT_NEG_MAX)
                for m in range(2):
                    b = 2 * z + m
                    last = nc.scalar.activation(probs[:, b], half_bank[z][0][:, T * m:T * m + T], ACT.Exp,
                                                bias=neg_max[:, b:b + 1], accum_out=prob_sum[:, b:b + 1])
                last.then_inc(half_out[z], 1)

            def half_probsT(z):
                act.wait_ge(half_mm[z], MM_PT)
                nc.scalar.copy(probsT[:, 2 * z:2 * z + 2],
                               half_bank[z][1][:, 0:2 * T].rearrange("p (b t) -> p b t", b=2)).then_inc(half_out[z], 1)

            half_rows(0, TO_X2T)
            half_probs(0)
            half_rows(1, TO_X2T)
            half_probsT(0)
            half_probs(1)
            half_probsT(1)
            half_rows(0, TO_X3T)
            half_rows(1, TO_X3T)
            for s in range(5, H):
                for place in ("first", "alpha", "q", "k", "last"):
                    tail_part(NG, s, place)

        @block.vector
        def _(dve):
            def wait_first(s, value):
                dve.wait_ge(s, value)
                nc.vector.memset(scratch[:], 0.0)

            def ln_stats(i, k, src, half=None):
                for b in range(GB) if half is None else (2 * half, 2 * half + 1):
                    last = nc.vector.bn_stats(stats[:, b], src[:, b])
                if half != 0:
                    last.then_inc(ln_stat, 1)

            def ln_variance(i, k):
                base = norms_done(i, k)
                wait_first(ln_stat, 2 * base + 1)
                for b in range(GB):
                    last = nc.vector.bn_aggr(mean_var[:, b], stats[:, b])
                last.then_inc(ln_stat, 1)
                dve.wait_ge(ln_stat, 2 * base + 2)
                nc.vector.tensor_scalar(var_eps[:], mean_var[:, :, 1], LN_EPS, None, ALU.add).then_inc(ln_var, 1)

            def ln_normalize(i, k, src):
                dve.wait_ge(ln_rstd, norms_done(i, k) + 1)
                if k > 0:
                    f = (None, XT1, X2T1)[k]
                    if not (isinstance(i, int) and i == NG and k == 1):
                        dve.wait_ge(tail_mm[1], fills(i, f) + 1)
                for b in range(GB):
                    last = nc.vector.tensor_scalar(xn[:, b], src[:, b], mean_var[:, b, 0:1], rstd[:, b:b + 1],
                                                   ALU.subtract, ALU.mult)
                last.then_inc(ln_out, 1)

            def decay(n, par, l):
                w = 2 ** (l - 1)
                m = N // (2 * w)
                src = spans if l > 1 else alpha
                off = (0 if l > 1 else par * N) + (0 if l < 3 else 2 * (N // 2 - N // 2 ** (l - 1)))
                pair = view(qk_dec, par * 2 * N + w, [[N - w, 2], [2 * w, m], [1, w]])
                other = view(src, off, [[1, 2], [2, m], [0, w]])
                dve.wait_ge(level_mm, LEVELS * n + l)
                dve.wait_ge(k_set, n + 1) if l == 1 else dve.wait_ge(span_set, 5 * n + l - 1)
                dve.wait_ge(level0_set, n + 1) if l == 1 else dve.wait_ge(decayed, OUTER * n + l - 1)
                nc.vector.tensor_tensor(pair, pair, other, ALU.mult).then_inc(decayed, 1)
                if l < LEVELS - 1:
                    to = 2 * (N // 2 - N // 2 ** l)
                    nc.vector.tensor_tensor(spans[:, to:to + m], view(src, off, [[2, m]]),
                                            view(src, off + 1, [[2, m]]), ALU.mult).then_inc(span_set, 1)

            def mask(n, half):
                slots = slice(0, 4) if half == 0 else slice(4, 6)
                of_bank = (bank_lo, bank_hi)[half][:, 0:(4 if half == 0 else 2) * N_IN]
                dve.wait_ge(level_mm, LEVELS * n + (3 if half == 0 else 5))
                nc.vector.tensor_tensor(by_level[:, slots].rearrange("p l b t -> p l (b t)"),
                                        of_bank.rearrange("p (l m) -> p l m", m=N_IN),
                                        owned[:, slots], ALU.mult).then_inc(masked, 1)
                if half == 1:
                    dve.wait_ge(masked, 2 * n + 2)
                    positive(dve, attnT_set, n)
                    nc.vector.tensor_reduce(blocks[:].rearrange("p b t -> p (b t)"),
                                            by_level[:].rearrange("p l b t -> p (b t) l"), AX,
                                            ALU.add).then_inc(blocks_set, 1)

            def squares_in(n):
                dve.wait_ge(norm_mm, n + 1)
                positive(dve, rnorm_set, n)
                nc.vector.tensor_tensor(self_diag[:].rearrange("p (a b) t -> p a (b t)", a=2),
                                        bank_k[:, 0:2 * N_IN].rearrange("p (a m) -> p a m", a=2),
                                        owned[:, 0:1].broadcast_to([P, 2, N_IN]), ALU.mult).then_inc(self_set, 1)
                dve.wait_ge(self_set, 2 * n + 1)
                nc.vector.tensor_reduce(self_sq[:], self_diag[:], AX, ALU.add).then_inc(self_set, 1)
                dve.wait_ge(self_set, 2 * n + 2)
                nc.vector.tensor_scalar(norm_sq[:].rearrange("p a b -> p (a b)"), self_sq[:],
                                        NORM_EPS * NORM_EPS, None, ALU.max).then_inc(norm_sq_set, 1)

            def o_scaled(n, par):
                dve.wait_ge(o_mm, n + 1)
                positive(dve, oT_mm, n)
                nc.vector.tensor_tensor(o_sb[:], bank_o[:].rearrange("p (b v) -> p b v", b=GB),
                                        rnorm[:, par, 0].unsqueeze(2).broadcast_to([P, GB, P]),
                                        ALU.mult).then_inc(o_set, 1)

            def softmaxed_gate(i, part):
                count = [SMALL * (i - 1) + (0, 5, 9)[part]]

                def link(ins, plain=False):
                    ins.then_inc(small, 1)
                    count[0] = count[0] + 1
                    (wait_first if plain else dve.wait_ge)(small, count[0])

                def wide(a):
                    return a.unsqueeze(2).broadcast_to([P, GB, E])

                if part == 0:
                    dve.wait_ge(gate_exp_set, i)
                    link(nc.vector.tensor_reduce(gate_sum[:], gate_exp[:], AX, ALU.add))
                    link(nc.vector.reciprocal(gate_sum[:], gate_sum[:]))
                    link(nc.vector.tensor_tensor(gate_exp[:], gate_exp[:], wide(gate_sum[:]), ALU.mult), True)
                    for b in range(GB):
                        ins = nc.vector.max(top_val[:, b], gate_exp[:, b])
                    link(ins, True)
                    for b in range(GB):
                        ins = nc.vector.max_index(top_idx[:, b], top_val[:, b], gate_exp[:, b])
                    link(ins)
                if part == 1:
                    link(nc.vector.tensor_copy(top_num[:], top_idx[:]))
                    every = experts[:].unsqueeze(1).broadcast_to([P, GB, E])
                    nc.vector.tensor_tensor(is_first[:], every, top_num[:, :, 0:1].broadcast_to([P, GB, E]),
                                            ALU.is_equal)
                    nc.vector.tensor_tensor(is_second[:], every, top_num[:, :, 1:2].broadcast_to([P, GB, E]),
                                            ALU.is_equal)
                    link(nc.vector.tensor_tensor(top_sum[:], top_val[:, :, 0], top_val[:, :, 1], ALU.add))
                    nc.vector.tensor_scalar(top_sum[:], top_sum[:], TOPW_EPS, None, ALU.add)
                    link(nc.vector.tensor_tensor(is_first[:], is_first[:], is_second[:], ALU.add))
                    nc.vector.reciprocal(top_sum[:], top_sum[:])
                    link(nc.vector.tensor_tensor(weight[:], gate_exp[:], is_first[:], ALU.mult))
                if part == 2:
                    link(nc.vector.tensor_tensor(weight[:], weight[:], wide(top_sum[:]), ALU.mult))
                    pairs = weight[:].rearrange("p b (j e) -> p j b e", e=2)
                    nc.vector.tensor_copy(weight_col[0:64], pairs[0:64, :, :, 0])
                    link(nc.vector.tensor_copy(weight_col[64:P], pairs[64:P, :, :, 1]))

            def residual(i):
                dve.wait_ge(x_res_set, i)
                for f in (WO0, WO1):
                    k = f - WO0
                    dve.wait_ge(tail_mm[k], fills(i, f) + 1)
                    nc.vector.tensor_tensor(x_mid[:, 2 * k:2 * k + 2],
                                            tails[k][:].rearrange("p (b d) -> p b d", b=2),
                                            x_res[:, 2 * k:2 * k + 2], ALU.add).then_inc(tail_free[k], 1)

            def cross_residual(i, f):
                dve.wait_ge(tail_mm[f % 2], fills(i, f) + 1)
                for m in range(2):
                    b = 2 * (f - AV0) + m
                    ins = nc.vector.scalar_tensor_tensor(
                        out=x_mid[:, b], in0=tails[f % 2][:, D * m:D * m + D], scalar=prob_rsum[:, b:b + 1],
                        in1=x_mid[:, b], op0=ALU.mult, op1=ALU.add)
                ins.then_inc(tail_free[f % 2], 1)

            def last_residual(i, f):
                dve.wait_ge(out_free, 16 * i)
                k = f - UPA
                dve.wait_ge(tail_mm[f % 2], fills(i, f) + 1)
                nc.vector.tensor_tensor(out_sb[:, 2 * k:2 * k + 2],
                                        tails[f % 2][:].rearrange("p (b d) -> p b d", b=2),
                                        x_mid[:, 2 * k:2 * k + 2], ALU.add).then_inc(tail_free[f % 2], 1)

            def gate_products():
                nc.vector.tensor_tensor(gated[:], pooled[:].unsqueeze(3).broadcast_to([P, KC, GB, E]),
                                        gate_sb[:].unsqueeze(2).broadcast_to([P, KC, GB, E]),
                                        ALU.mult).then_inc(gated_set, 1)

            def weigh(i, j):
                dve.wait_ge(tail_free[(H0 + j) % 2], fills(i, H0 + j) + 1)
                dve.wait_ge(small, SMALL * i)
                hj = hidden[:, j].rearrange("p (b t) -> p b t", b=GB)
                nc.vector.tensor_tensor(hj, hj, weight_col[:, j].unsqueeze(2).broadcast_to([P, GB, T]),
                                        ALU.mult).then_inc(weighted, 1)

            def tail_part(i, s, slot):
                at = (s, slot)
                if at == (0, 1):
                    for f in (WO0, WO1):
                        dve.wait_ge(tail_free[f % 2], fills(i, f) + 1)
                if s == 0 and slot in (1, 2):
                    ln_stats(i, 1, x_mid, slot - 1)
                if at == (0, 3):
                    ln_variance(i, 1)
                if at == (0, 6):
                    ln_normalize(i, 1, x_mid)
                if at == (1, 6):
                    dve.wait_ge(tail_mm[0], fills(i, SCORES) + 1)
                    nc.vector.tensor_reduce(row_max[:], tail0[:].rearrange("p (b t) -> p b t", b=GB), AX,
                                            ALU.max).then_inc(row_stat, 1)
                    dve.wait_ge(row_stat, 2 * (i - 1) + 1)
                    nc.vector.tensor_scalar(neg_max[:], row_max[:], -1.0, None, ALU.mult).then_inc(max_set, 1)
                if at == (2, 3):
                    dve.wait_ge(tail_free[0], fills(i, SCORES) + 1)
                    nc.vector.reciprocal(prob_rsum[:], prob_sum[:]).then_inc(row_stat, 1)
                if at == (2, 6):
                    dve.wait_ge(row_stat, 2 * (i - 1) + 2)
                    cross_residual(i, AV0)
                if at == (3, 0):
                    cross_residual(i, AV1)
                if at == (3, 1):
                    for f in (AV0, AV1):
                        dve.wait_ge(tail_free[f % 2], fills(i, f) + 1)
                if s == 3 and slot in (1, 2):
                    ln_stats(i, 2, x_mid, slot - 1)
                if at == (3, 3):
                    ln_variance(i, 2)
                if at == (3, 6):
                    ln_normalize(i, 2, x_mid)
                if s == 4 and slot in (3, 5):
                    c = (slot - 3) // 2
                    dve.wait_ge(x3T_hi, KC * (i - 1) + c + 1)
                    nc.vector.tensor_reduce(pooled[:, c],
                                            tails[c][:].rearrange("p (b t) -> p b t", b=GB), AX,
                                            ALU.add).then_inc(pooled_set, 1)
                if s == 4 and slot in (4, 6):
                    c = (slot - 4) // 2
                    nc.vector.tensor_tensor(x3T[:, LO, c], tails[c][:], x3T[:, HI, c].bitcast(F32),
                                            ALU.subtract).then_inc(tail_free[c], 1)
                if at == (4, 6):
                    dve.wait_ge(pooled_set, KC * i)
                    gate_products()
                if at == (5, 2):
                    dve.wait_ge(tail_mm[0], fills(i, GATE) + 1)
                    nc.vector.tensor_scalar(logits[:].rearrange("p b e -> p (b e)"), tail0[:, 0:GB * E], 1.0 / T, None,
                                            ALU.mult).then_inc(tail_free[0], 1)
                    dve.wait_ge(tail_free[0], fills(i, GATE) + 1)
                    nc.vector.tensor_reduce(gate_max[:], logits[:], AX, ALU.max).then_inc(gate_max_set, 1)
                    dve.wait_ge(gate_max_set, i)
                    nc.vector.tensor_tensor(logits[:], logits[:], gate_max[:].unsqueeze(2).broadcast_to([P, GB, E]),
                                            ALU.subtract).then_inc(logits_set, 1)
                if at == (5, 6):
                    softmaxed_gate(i, 0)
                if s == 6 and slot in (1, 2):
                    softmaxed_gate(i, slot)
                if at == (7, 0):
                    dve.wait_ge(tail_mm[1], fills(i, WT) + 1)
                    nc.vector.tensor_copy(weightT[:].rearrange("e b t -> e (b t)"),
                                          tail1[0:E, :]).then_inc(tail_free[1], 1)
                if at == (7, 3):
                    last_residual(i, UPA)
                if at == (7, 5):
                    last_residual(i, UPB)

            def split_weights(k):
                dve.wait_ge(w_hi, k + 1)
                parts, whole = staged[k]
                upper = parts[:, HI].bitcast(F32).rearrange("p c n -> p (c n)")
                nc.vector.tensor_tensor(parts[:, LO].rearrange("p c n -> p (c n)"), whole, upper,
                                        ALU.subtract).then_inc(w_split, 1)

            def xnT_lower(i):
                for c in range(KC):
                    dve.wait_ge(xT_hi, KC * i + c + 1)
                    nc.vector.tensor_tensor(xnT[:, LO, c], tails[c][:], xnT[:, HI, c].bitcast(F32),
                                            ALU.subtract).then_inc(tail_free[c], 1)

            def next_x(i, slot):
                if slot == 1:
                    dve.wait_ge(x_in, 16 * (i + 1))
                if slot in (1, 2):
                    ln_stats(i, 0, x_next, slot - 1)
                if slot == 3:
                    ln_variance(i, 0)
                if slot == 4:
                    ln_normalize(i, 0, x_next)

            def body(i, tail, last=False):
                if tail:
                    o_scaled(i * H - 1, (H - 1) % 2)
                squares_in(i * H)
                if tail:
                    residual(i)
                for h in range(H):
                    n, par, more = i * H + h, h % 2, h < H - 1
                    if tail:
                        tail_part(i, h, 0)
                    for l in range(1, LEVELS):
                        decay(n, par, l)
                        if l == 3:
                            mask(n, 0)
                        if l == 5 and h > 0:
                            o_scaled(n - 1, 1 - par)
                        if l == 6 and not tail and h == H - 2:
                            split_weights(DOWN)
                        if l == 6 and not more and not last:
                            xnT_lower(i + 1)
                        if l == 6:
                            mask(n, 1)
                        if l == 6 and more:
                            squares_in(n + 1)
                        if tail:
                            tail_part(i, h, l)
                        if not more and not last:
                            next_x(i + 1, l)

            for slot in range(1, 5):
                next_x(0, slot)
            split_weights(0)
            xnT_lower(0)
            for k in range(1, 4):
                split_weights(k)
            dve.wait_ge(c_in, N_C)
            body(0, False)
            dve.wait_ge(w_in, N_W)
            with dve.Fori(1, NG - 1) as i:
                body(i, True)
            body(NG - 1, True, last=True)
            o_scaled(NG * H - 1, (H - 1) % 2)

            def done(ins, z):
                ins.then_inc(half_row[z], 1)

            def half_mid(z, step):
                dve.wait_ge(half_mm[z], MM_WO if step == AT_MID else MM_AV)
                two = slice(2 * z, 2 * z + 2)
                if step == AT_MID:
                    dve.wait_ge(x_res_set, NG)
                    done(nc.vector.tensor_tensor(x_mid[:, two], half_bank[z][0][:].rearrange("p (b d) -> p b d", b=2),
                                                 x_res[:, two], ALU.add), z)
                else:
                    dve.wait_ge(half_row[z], AT_RSUM)
                    for m in range(2):
                        b = 2 * z + m
                        ins = nc.vector.scalar_tensor_tensor(
                            out=x_mid[:, b], in0=half_bank[z][0][:, D * m:D * m + D], scalar=prob_rsum[:, b:b + 1],
                            in1=x_mid[:, b], op0=ALU.mult, op1=ALU.add)
                    done(ins, z)
                dve.wait_ge(half_row[z], step)
                for b in (2 * z, 2 * z + 1):
                    ins = nc.vector.bn_stats(stats[:, b], x_mid[:, b])
                done(ins, z)
                dve.wait_ge(half_row[z], step + 1)
                for b in (2 * z, 2 * z + 1):
                    ins = nc.vector.bn_aggr(mean_var[:, b], stats[:, b])
                done(ins, z)
                dve.wait_ge(half_row[z], step + 2)
                done(nc.vector.tensor_scalar(var_eps[:, two], mean_var[:, two, 1], LN_EPS, None, ALU.add), z)

            def half_xn(z, count):
                dve.wait_ge(half_rstd[z], count)
                for b in (2 * z, 2 * z + 1):
                    ins = nc.vector.tensor_scalar(xn[:, b], x_mid[:, b], mean_var[:, b, 0:1], rstd[:, b:b + 1],
                                                  ALU.subtract, ALU.mult)
                done(ins, z)

            def half_max(z):
                two = slice(2 * z, 2 * z + 2)
                dve.wait_ge(half_mm[z], MM_SCORES)
                scores = half_bank[z][0][:, 0:2 * T].rearrange("p (b t) -> p b t", b=2)
                done(nc.vector.tensor_reduce(row_max[:, two], scores, AX, ALU.max), z)
                dve.wait_ge(half_row[z], AT_MAX)
                done(nc.vector.tensor_scalar(neg_max[:, two], row_max[:, two], -1.0, None, ALU.mult), z)

            def half_rsum(z):
                two = slice(2 * z, 2 * z + 2)
                dve.wait_ge(half_out[z], TO_PROBS)
                done(nc.vector.reciprocal(prob_rsum[:, two], prob_sum[:, two]), z)

            def half_pooled(z):
                cols = slice(2 * T * z, 2 * T * z + 2 * T)
                src = half_bank[z][1][:]
                dve.wait_ge(half_out[z], TO_X3T)
                done(nc.vector.tensor_reduce(pooled[:, :, 2 * z:2 * z + 2],
                                             src.rearrange("p (c b t) -> p c b t", c=KC, b=2), AX, ALU.add), z)
                done(nc.vector.tensor_tensor(x3T[:, LO, :, cols], src.rearrange("p (c n) -> p c n", c=KC),
                                             x3T[:, HI, :, cols].bitcast(F32), ALU.subtract), z)

            half_mid(0, AT_MID)
            half_xn(0, 1)
            half_mid(1, AT_MID)
            half_xn(1, 1)
            half_max(0)
            half_rsum(0)
            half_max(1)
            half_mid(0, AT_MID2)
            half_rsum(1)
            half_xn(0, 2)
            half_mid(1, AT_MID2)
            half_xn(1, 2)
            half_pooled(0)
            half_pooled(1)
            dve.wait_ge(half_row[0], AT_POOLED)
            dve.wait_ge(half_row[1], AT_POOLED)
            gate_products()
            for s in range(5, H):
                if s == H - 1:
                    for j in range(EJ // 2, EJ):
                        weigh(NG, j)
                for slot in range(LEVELS):
                    tail_part(NG, s, slot)

        @block.tensor
        def _(pe):
            mm = nc.tensor.matmul
            PARTS = ((HI, HI), (HI, LO), (LO, HI))

            def project(w, dst, h):
                for c in range(KC):
                    for k, (a, b) in enumerate(PARTS):
                        last = mm(dst[:], w[:, a, c, P * h:P * h + P], xnT[:, b, c], start=(c == 0 and k == 0),
                                  stop=(c == KC - 1 and k == 2))
                return last

            def project_g(i, h):
                n = i * H + h
                positive(pe, v_raw_set, n + (1 if h > 0 else 0))
                project(wg_sb, bank_gv, h).then_inc(g_mm, 1)

            def project_q(n, h):
                positive(pe, attnT_set, n - (1 if h > 0 else 0))
                project(wq_sb, bank_q, h).then_inc(q_mm, 1)

            def project_k(n, h):
                positive(pe, norm_sq_set, n)
                project(wk_sb, bank_k, h).then_inc(k_mm, 1)

            def project_v(i, m):
                pair, half = m // 2, m % 2
                if m != 1:
                    pe.wait_ge(alpha_set, i * H + max(m, 1))
                else:
                    pe.wait_ge(v_raw_set, i * H + 1)
                for k in range(2):
                    b = 2 * half + k
                    for c in range(KC):
                        for part, (a, w) in enumerate(PARTS):
                            last = mm(bank_gv[:, 2 * P * k:2 * P * k + 2 * P], xnT[:, a, c, T * b:T * b + T],
                                      wv_sb[:, w, c, 2 * P * pair:2 * P * pair + 2 * P],
                                      start=(c == 0 and part == 0), stop=(c == KC - 1 and part == 2))
                last.then_inc(v_mm, 1)

            def norms(n, par):
                pe.wait_ge(q_set, n + 1)
                pe.wait_ge(k_set, n + 1)
                block_products(bank_k, 0, q_raw[:, par], q_raw[:, par])
                block_products(bank_k, 1, qk_dec[:, par, 1], qk_dec[:, par, 1]).then_inc(norm_mm, 1)

            def block_products(dst, slot, left, right):
                for b in range(GB):
                    for r in range(T // BLOCK):
                        at = T * b + BLOCK * r
                        to = slot * GB * BLOCK + b * BLOCK
                        last = mm(dst[BLOCK * r:BLOCK * r + BLOCK, to:to + BLOCK], left[:, at:at + BLOCK],
                                  right[:, at:at + BLOCK], start=True, stop=True)
                return last

            def level(n, par, l, more):
                q, k = qk_dec[:, par, 0], qk_dec[:, par, 1]
                if l > 0:
                    pe.wait_ge(decayed, OUTER * n + l)
                if l == 0:
                    pe.wait_ge(level0_set, n + 1)
                    pe.wait_ge(k_set, n + 1)
                    pe.wait_ge(q_set, n + 1)
                    positive(pe, masked, 2 * n)
                    block_products(bank_lo, 0, k, q_raw[:, par])
                    last = block_products(bank_lo, 1, k, q)
                elif l < 3:
                    last = block_products(bank_lo, l + 1, k, q)
                elif l < INNER:
                    last = block_products(bank_hi, l - 3, k, q)
                else:
                    if l == INNER:
                        pe.wait_ge(q_set, n + (2 if more else 1))
                    w = 2 ** l
                    for b in range(GB):
                        for s in range(0, T, 2 * w):
                            at, to = T * b + s, (0 if l == INNER else GB * BLOCK) + w * b
                            last = mm(bank_q[s:s + w, to:to + w], k[:, at:at + w], q[:, at + w:at + 2 * w],
                                      start=True, stop=True)
                last.then_inc(level_mm, 1)

            def attend(n, par):
                positive(pe, oT_set, n)
                pe.wait_ge(attnT_set, n + 1)
                pe.wait_ge(v_set, n + 1)
                for b in range(GB):
                    last = mm(bank_o[:, P * b:P * b + P], attnT[:, b], v_sb[:, par, b], start=True, stop=True)
                last.then_inc(o_mm, 1)

            def attend_transposed(n):
                pe.wait_ge(o_set, n + 1)
                for b in range(GB):
                    last = nc.tensor.transpose(bank_o[:, P * b:P * b + P], o_sb[:, b], ident[:])
                last.then_inc(oT_mm, 1)

            def fill(i, f):
                positive(pe, tail_free[f % 2], fills(i, f))
                return tails[f % 2]

            def transposed(i, f0):
                for c in range(KC):
                    dst = fill(i, f0 + c)
                    for b in range(GB):
                        last = nc.tensor.transpose(dst[:, T * b:T * b + T], xn[:, b, P * c:P * c + P], ident[:])
                    last.then_inc(tail_mm[(f0 + c) % 2], 1)

            def cross_keys(i, f):
                j = f % 2
                pe.wait_ge(ctxT_in, 16 * KC * (i + 1))
                dst = fill(i, f)
                for c in range(KC):
                    last = mm(dst[:], xw_sb[:, c, P * j:P * j + P], ctxT_sb[:, c].rearrange("p b t -> p (b t)"),
                              start=(c == 0), stop=(c == KC - 1))
                last.then_inc(tail_mm[j], 1)

            def output_projection(i):
                pe.wait_ge(oT_set, H * i)
                for f in (WO0, WO1):
                    dst = fill(i, f)
                    for m in range(2):
                        b = 2 * (f - WO0) + m
                        for h in range(H):
                            last = mm(dst[:, D * m:D * m + D], oT_sb[:, h, T * b:T * b + T], wo_sb[:, h],
                                      start=(h == 0), stop=(h == H - 1))
                    last.then_inc(tail_mm[f % 2], 1)

            def up_projection(i, b):
                f, m = UPA + b // 2, b % 2
                dst = tails[f % 2]
                if m == 0:
                    pe.wait_ge(weighted, EJ * i)
                    pe.wait_ge(tail_free[1], fills(i, WT) + 1)
                    fill(i, f)
                for j in range(EJ):
                    mm(dst[:, D * m:D * m + D], hidden[:, j, T * b:T * b + T], up_sb[:, j],
                       start=(j == 0), stop=False)
                last = mm(dst[:, D * m:D * m + D], weightT[:, b], upb_sb[:], start=False, stop=True)
                if m == 1:
                    last.then_inc(tail_mm[f % 2], 1)

            def hidden_units(i, f):
                j = f - H0
                dst = fill(i, f)
                for c in range(KC):
                    for k, (a, b) in enumerate(PARTS):
                        last = mm(dst[:], down_sb[:, a, c, P * j:P * j + P], x3T[:, b, c],
                                  start=(c == 0 and k == 0), stop=(c == KC - 1 and k == 2))
                last.then_inc(tail_mm[f % 2], 1)

            def tail_part(i, s, l):
                at = (s, l)
                if at == (1, 1) or at == (4, 1):
                    pe.wait_ge(ln_out, norms_done(i, 1 if s == 1 else 2) + 1)
                    transposed(i, X2T0 if s == 1 else X3T0)
                if at == (1, 3):
                    pe.wait_ge(tail_free[0], fills(i, X2T0) + 1)
                    pe.wait_ge(tail_free[1], fills(i, X2T1) + 1)
                    dst = fill(i, SCORES)
                    for b in range(GB):
                        for c in range(KC):
                            last = mm(dst[:, T * b:T * b + T], x2T[:, c, T * b:T * b + T], projT[:, c, b],
                                      start=(c == 0), stop=(c == KC - 1))
                    last.then_inc(tail_mm[0], 1)
                if at == (2, 2):
                    pe.wait_ge(tail_free[0], fills(i, SCORES) + 1)
                    dst = fill(i, PT)
                    for b in range(GB):
                        last = nc.tensor.transpose(dst[:, T * b:T * b + T], probs[:, b], ident[:])
                    last.then_inc(tail_mm[1], 1)
                if at == (2, 4):
                    pe.wait_ge(tail_free[1], fills(i, PT) + 1)
                    pe.wait_ge(ctx_in, 16 * i)
                    for f in (AV0, AV1):
                        dst = fill(i, f)
                        for m in range(2):
                            b = 2 * (f - AV0) + m
                            last = mm(dst[:, D * m:D * m + D], probsT[:, b], ctx_sb[:, b], start=True, stop=True)
                        last.then_inc(tail_mm[f % 2], 1)
                if at == (5, 1):
                    if not (isinstance(i, int) and i == NG):
                        pe.wait_ge(tail_free[0], fills(i, X3T0) + 1)
                    hidden_units(i, H0)
                if at == (5, 1):
                    pe.wait_ge(gated_set, i)
                    dst = fill(i, GATE)
                    for c in range(KC):
                        last = mm(dst[:, 0:GB * E], ones[:].broadcast_to([P, P]),
                                  gated[:, c].rearrange("p b e -> p (b e)"), start=(c == 0), stop=(c == KC - 1))
                    last.then_inc(tail_mm[0], 1)
                if at == (5, 6):
                    for f in (H1, H2, H3):
                        hidden_units(i, f)
                if at == (6, 5) and not (isinstance(i, int) and i == NG):
                    cross_keys(i, KEY0)
                if at == (6, 6):
                    pe.wait_ge(small, SMALL * i)
                    dst = fill(i, WT)
                    for b in range(GB):
                        last = nc.tensor.transpose(dst[0:E, T * b:T * b + T], weight[:, b], ident[:])
                    last.then_inc(tail_mm[1], 1)

            def normalized(i):
                pe.wait_ge(ln_out, norms_done(i, 0) + 1)
                transposed(i, XT0)

            def body(i, tail, first=False, last=False):
                n = i * H
                pe.wait_ge(tail_free[1], fills(i, XT1) + 1)
                pe.wait_ge(tail_free[0], fills(i, XT0) + 1)
                if first:
                    pe.wait_ge(w_split, 1)
                project_g(i, 0)
                if first:
                    pe.wait_ge(w_split, 2)
                    project_q(n, 0)
                    pe.wait_ge(w_split, 3)
                project_k(n, 0)
                if tail:
                    attend(n - 1, (H - 1) % 2)
                    project_q(n, 0)
                if tail:
                    attend_transposed(n - 1)
                if first:
                    pe.wait_ge(w_split, 4)
                project_v(i, 0)
                norms(n, 0)
                project_v(i, 1)
                if tail:
                    output_projection(i)
                for h in range(H):
                    n, par, more = i * H + h, h % 2, h < H - 1
                    up = tail and not more
                    for l in range(LEVELS):
                        level(n, par, l, more)
                        if l == 6 and h > 0:
                            attend_transposed(n - 1)
                        if tail:
                            tail_part(i, h, l)
                        if l == 0 and more:
                            project_g(i, h + 1)
                        if l == 1 and more:
                            project_q(n + 1, h + 1)
                        if l == 2 and more:
                            project_k(n + 1, h + 1)
                        if l == 3 and h > 0:
                            attend(n - 1, 1 - par)
                        if l == 4 and more:
                            norms(n + 1, 1 - par)
                        if l == 5 and h + 2 < H:
                            project_v(i, h + 2)
                        if up and l in (0, 1, 2, 4):
                            up_projection(i, min(l, 3))
                        if not (tail or more) and l == 0:
                            pe.wait_ge(w_in, N_W)
                            cross_keys(i, KEY0)
                        if not more and l == (5 if tail else 2):
                            cross_keys(i, KEY1)
                        if l == 5 and not (more or last):
                            normalized(i + 1)

            pe.wait_ge(ident_in, 16)
            pe.wait_ge(consts_set, 1)
            normalized(0)
            body(0, False, first=True)
            with pe.Fori(1, NG - 1) as i:
                body(i, True)
            body(NG - 1, True, last=True)

            def half_wo(b, heads):
                z, m = b // 2, b % 2
                for h in heads:
                    ins = mm(half_bank[z][0][:, D * m:D * m + D], oT_sb[:, h, T * b:T * b + T], wo_sb[:, h],
                             start=(h == 0), stop=(h == H - 1))
                if m == 1 and heads[-1] == H - 1:
                    ins.then_inc(half_mm[z], 1)

            def half_transposed(z, step):
                pe.wait_ge(half_row[z], AT_XN if step == MM_X2T else AT_XN2)
                for c in range(KC):
                    for m in range(2):
                        to = 2 * T * c + T * m
                        last = nc.tensor.transpose(half_bank[z][1][:, to:to + T], xn[:, 2 * z + m, P * c:P * c + P],
                                                   ident[:])
                last.then_inc(half_mm[z], 1)

            def half_scores(z):
                pe.wait_ge(half_out[z], TO_X2T)
                for m in range(2):
                    b = 2 * z + m
                    for c in range(KC):
                        last = mm(half_bank[z][0][:, T * m:T * m + T], x2T[:, c, T * b:T * b + T], projT[:, c, b],
                                  start=(c == 0), stop=(c == KC - 1))
                last.then_inc(half_mm[z], 1)

            def half_probsT(z):
                pe.wait_ge(half_out[z], TO_PROBS)
                for m in range(2):
                    last = nc.tensor.transpose(half_bank[z][1][:, T * m:T * m + T], probs[:, 2 * z + m], ident[:])
                last.then_inc(half_mm[z], 1)

            def half_context(z):
                pe.wait_ge(half_out[z], TO_PT)
                for m in range(2):
                    b = 2 * z + m
                    last = mm(half_bank[z][0][:, D * m:D * m + D], probsT[:, b], ctx_sb[:, b], start=True, stop=True)
                last.then_inc(half_mm[z], 1)

            every = range(H)
            pe.wait_ge(norm_sq_set, H * NG)
            pe.wait_ge(oT_set, H * NG - 2)
            half_wo(0, every[:6])
            attend(NG * H - 1, (H - 1) % 2)
            pe.wait_ge(oT_set, H * NG - 1)
            half_wo(0, every[6:7])
            half_wo(2, every[:3])
            attend_transposed(NG * H - 1)
            half_wo(2, every[3:7])
            pe.wait_ge(oT_set, H * NG)
            pe.wait_ge(ctx_in, 16 * NG)
            half_wo(0, every[7:])
            half_wo(1, every)
            half_wo(2, every[7:])
            half_wo(3, every[:7])
            half_transposed(0, MM_X2T)
            half_wo(3, every[7:])
            half_scores(0)
            half_transposed(1, MM_X2T)
            half_probsT(0)
            half_scores(1)
            half_context(0)
            half_probsT(1)
            half_context(1)
            half_transposed(0, MM_X3T)
            half_transposed(1, MM_X3T)
            for z in range(2):
                pe.wait_ge(half_row[z], AT_X3T)
            for s in range(5, H):
                for l in range(LEVELS):
                    tail_part(NG, s, l)
            for b in range(GB):
                up_projection(NG, b)


def kernel(x, ctx_1024, L0_attn_Wq, L0_attn_Wk, L0_attn_Wv, L0_attn_Wg, L0_attn_Wo, L0_xattn_W,
           L0_ffn_gate_w, L0_ffn_down_w, L0_ffn_down_b, L0_ffn_up_w, L0_ffn_up_b):
    import concourse.bacc as bacc
    from concourse.bass_utils import run_bass_kernel_spmd

    E, BN, D = L0_ffn_down_w.shape
    ident, owned, experts = shape_constants(4)
    arrays = {
        "x": x,
        "ctx": ctx_1024,
        "ctxT": np.transpose(ctx_1024, (0, 2, 1)),
        "wq": L0_attn_Wq, "wk": L0_attn_Wk, "wv": L0_attn_Wv, "wg": L0_attn_Wg, "wo": L0_attn_Wo,
        "xwT": np.transpose(L0_xattn_W),
        "gateT": np.transpose(L0_ffn_gate_w),
        "downT": np.transpose(np.reshape(L0_ffn_down_w, (E * BN, D))),
        "down_b": np.transpose(np.reshape(L0_ffn_down_b, (E * BN // P, P))),
        "up": np.reshape(np.transpose(L0_ffn_up_w, (0, 2, 1)), (E * BN, D)),
        "up_b": L0_ffn_up_b,
        "ident_c": ident, "owned_c": owned, "experts_c": experts,
    }
    arrays = {name + "_dram": np.ascontiguousarray(a) for name, a in arrays.items()}
    nc = bacc.Bacc("TRN2", target_bir_lowering=False, num_devices=1)
    args = [nc.dram_tensor(name, a.shape, mybir.dt.from_np(a.dtype), kind="ExternalInput").ap()
            for name, a in arrays.items()]
    out = nc.dram_tensor("out_dram", x.shape, F32, kind="ExternalOutput").ap()
    decoder_kernel(nc, *args, out)
    r = run_bass_kernel_spmd(nc, [arrays], core_ids=[0])
    return r.results[0]["out_dram"]
```
